# Optimizing a Trainium2 kernel written in Bass

```python
import numpy as np
import jax
import jax.numpy as jnp

def _softmax(x, axis=-1):
    return jax.nn.softmax(x, axis=axis)

def _gelu(x):
    return jax.nn.gelu(x, approximate=True)

def _silu(x):
    return jax.nn.silu(x)

def _sigmoid(x):
    return jax.nn.sigmoid(x)

def _layernorm(x, axis=-1, eps=1e-05):
    m = jnp.mean(x, axis=axis, keepdims=True)
    v = jnp.var(x, axis=axis, keepdims=True)
    return (x - m) / jnp.sqrt(v + eps)

def _scatter_add(tgt, idx, src, axis=0):
    return tgt.at[idx].add(src)

def _segment_sum(src, seg, n):
    return jax.ops.segment_sum(src, seg, n)
kernel_name = 'mk_sandwich_d1_jaxref_r4_39c34b'

def setup_inputs(seed: int=0):
    np.random.seed(seed)
    _w = jnp.asarray

    def _L0_attn_setup():
        import jax, jax.numpy as jnp
        import numpy as np
        B, S, D = (1, 1024, 256)
        H, KVH = (16, 4)
        DH = D // H
        GROUPS = H // KVH
        SCALE = DH ** (-0.5)
        key = jax.random.key(seed)
        ks = jax.random.split(key, 5)
        std = D ** (-0.5)
        return {'x': jax.random.normal(ks[0], (B, S, D), dtype=jnp.float32), 'Wq': jax.random.normal(ks[1], (D, D), dtype=jnp.float32) * std, 'Wk': jax.random.normal(ks[2], (KVH * DH, D), dtype=jnp.float32) * std, 'Wv': jax.random.normal(ks[3], (KVH * DH, D), dtype=jnp.float32) * std, 'Wo': jax.random.normal(ks[4], (D, D), dtype=jnp.float32) * std}
    _L0_attn_in = _L0_attn_setup()

    def _L0_ffn_setup():
        import jax, jax.numpy as jnp
        import numpy as np
        R = 64
        key = jax.random.key(seed)
        k1, k2, k3 = jax.random.split(key, 3)
        B, S, D_IN, D_OUT = (8, 1024, 256, 256)
        x = jax.random.normal(k1, (B, S, D_IN), dtype=jnp.float32)
        weight = jax.random.normal(k2, (D_OUT, D_IN), dtype=jnp.float32) * (1.0 / np.sqrt(D_IN))
        disha = jax.random.normal(k3, (R, D_OUT), dtype=jnp.float32) * 0.01
        return {'x': x, 'weight': weight, 'disha': disha}
    _L0_ffn_in = _L0_ffn_setup()
    _d = {'L0_attn_x': _L0_attn_in['x'], 'L0_attn_Wq': _L0_attn_in['Wq'], 'L0_attn_Wk': _L0_attn_in['Wk'], 'L0_attn_Wv': _L0_attn_in['Wv'], 'L0_attn_Wo': _L0_attn_in['Wo'], 'L0_ffn_weight': _L0_ffn_in['weight'], 'L0_ffn_disha': _L0_ffn_in['disha']}
    _x0 = _d['L0_attn_x']
    _d['L0_attn_x'] = jax.random.normal(jax.random.fold_in(jax.random.key(seed), 1), (16, 512, 256), dtype=_x0.dtype)
    del _x0
    return _d

def reference(L0_attn_x, L0_attn_Wq, L0_attn_Wk, L0_attn_Wv, L0_attn_Wo, L0_ffn_weight, L0_ffn_disha):

    def _L0_attn_ref(x, Wq, Wk, Wv, Wo):
        import jax, jax.numpy as jnp
        import numpy as np
        B, S, D = (1, 1024, 256)
        H, KVH = (16, 4)
        DH = D // H
        GROUPS = H // KVH
        SCALE = DH ** (-0.5)
        b, s, _ = x.shape
        q = (x @ Wq.T).reshape(b, s, H, DH).transpose(0, 2, 1, 3)
        k = (x @ Wk.T).reshape(b, s, KVH, DH).transpose(0, 2, 1, 3)
        v = (x @ Wv.T).reshape(b, s, KVH, DH).transpose(0, 2, 1, 3)
        k = jnp.repeat(k, GROUPS, axis=1)
        v = jnp.repeat(v, GROUPS, axis=1)
        scores = jnp.einsum('bhqd,bhkd->bhqk', q, k) * SCALE
        causal = jnp.triu(jnp.full((s, s), -jnp.inf, dtype=scores.dtype), k=1)
        scores = scores + causal
        probs = jax.nn.softmax(scores, axis=-1)
        out = jnp.einsum('bhqk,bhkd->bhqd', probs, v)
        out = out.transpose(0, 2, 1, 3).reshape(b, s, D)
        return out @ Wo.T

    def _L0_ffn_ref(x, weight, disha):
        import jax, jax.numpy as jnp
        import numpy as np
        R = 64
        result = jnp.einsum('bsd,od->bso', x, weight)
        r = disha.shape[0]
        pooled = x.reshape(*x.shape[:-1], x.shape[-1] // r, r).sum(axis=-2)
        return result + pooled @ disha
    x = L0_attn_x
    x = x + _layernorm(_L0_attn_ref(_layernorm(x, axis=-1), L0_attn_Wq, L0_attn_Wk, L0_attn_Wv, L0_attn_Wo), axis=-1)
    x = x + _layernorm(_L0_ffn_ref(_layernorm(x, axis=-1), L0_ffn_weight, L0_ffn_disha), axis=-1)
    return x

_drawn_inputs = setup_inputs


def setup_inputs(seed=0):
    import zlib

    import numpy as np

    out = dict(_drawn_inputs(seed))
    spreads = {}
    factors = {}
    for name, (base, spread) in spreads.items():
        noise = np.random.default_rng([zlib.crc32(name.encode()), seed]).standard_normal(out[name].shape)
        drawn = base * np.exp(spread * noise) if base else spread * noise
        out[name] = jnp.asarray(drawn.astype(out[name].dtype))
    for name, factor in factors.items():
        out[name] = (out[name] * factor).astype(out[name].dtype)
    return out
```

```python
import concourse.bass as bass
from concourse import mybir
from contextlib import ExitStack


def sandwich_kernel(nc, x, wq, wk, wv, wo, wf, disha, out):
    F32, BF16 = mybir.dt.float32, mybir.dt.bfloat16
    ALU = mybir.AluOpType
    ACT = mybir.ActivationFunctionType
    AX = mybir.AxisListType

    B, S, D = x.shape
    H, DH, P = 16, 16, 128
    KVH = wk.shape[0] // DH
    HG = H // KVH
    R = disha.shape[0]
    NT = S // P
    NC = D // P
    SCALE = DH ** -0.5
    EPS = 1e-5
    NEG = -3.0e38
    HI, MID, LO = 0, 1, 2
    Q_PART = [HI, HI, MID, HI, MID, LO]
    K_PART = [HI, MID, HI, LO, MID, HI]
    KR = len(Q_PART) * DH
    KM = KR + 3
    ST = 10
    P1 = 11
    P1S = 3

    x_v = x.rearrange("b (t p) f -> b p t f", p=P)
    out_v = out.rearrange("b (t p) f -> b p t f", p=P)

    ctx = ExitStack()
    with ctx:
        def sb(name, shape, dt=F32):
            return ctx.enter_context(nc.sbuf_tensor(name, shape, dt))

        def sem(name):
            return ctx.enter_context(nc.semaphore(name))

        wq_sb = sb("wq_sb", [P, 2, D])
        wkv_sb = sb("wkv_sb", [P, D])
        wo_sb = sb("wo_sb", [P, 2, D])
        wo_perm = sb("wo_perm", [P, 2, D])
        wf_sb = sb("wf_sb", [P, 2, D])
        dish2 = sb("dish2", [P, D])
        wqT = sb("wqT", [P, NC, D])
        wkvT = sb("wkvT", [P, NC, P])
        woT = sb("woT", [P, NC, D])
        wfT = sb("wfT", [P, NC, D])
        identf = sb("identf", [P, P])
        identb = sb("identb", [P, P], BF16)
        causal = sb("causal", [P, P], BF16)
        powexp = sb("powexp", [P, NT])

        x_ln = sb("x_ln", [P, NT, D])
        xhat = sb("xhat", [P, NT, D])
        xT = sb("xT", [P, NC, S])
        q_split = sb("q_split", [P, 3, 2, S], BF16)
        k_split = sb("k_split", [64, 3, S], BF16)
        resid = sb("resid", [P, 3, S])
        vT_sb = sb("vT_sb", [P, S])
        QS = sb("QS", [P, 2, H, S], BF16)
        KS = sb("KS", [P, 2, KVH, S], BF16)
        V1 = sb("V1", [P, 2, NT, KVH, 2 * DH])

        mneg = sb("mneg", [P, 2, H])
        mres = sb("mres", [P, H])
        msplit = sb("msplit", [P, 3, H], BF16)
        mT_sb = sb("mT_sb", [3 * H, 2, P], BF16)
        PT = sb("PT", [P, 2 * ST, S])
        OT = sb("OT", [P, 2, KVH, S])

        zc = sb("zc", [P, 64])
        rc = sb("rc", [P, 64])
        r_dram = nc.dram_tensor("r_scratch", (HG, KVH * S), F32, kind="Internal").ap()
        rrep = sb("rrep", [P, NC, S])
        oraw = sb("oraw", [P, NC, S])
        oT = sb("oT", [P, NC, S])
        x_res = sb("x_res", [P, NT, D])
        tsum = sb("tsum", [P, NT, D])
        x2hat = sb("x2hat", [P, NT, D])
        x2T = sb("x2T", [P, NC, S])
        osum = sb("osum", [P, NT, D])
        outb = sb("outb", [P, NT, D])

        class Norm:
            def __init__(self, n):
                self.stats = sb(f"ln{n}_stats", [P, NT, 6])
                self.mv = sb(f"ln{n}_mv", [P, NT, 2])
                self.veps = sb(f"ln{n}_veps", [P, NT])
                self.rstd = sb(f"ln{n}_rstd", [P, NT])
                self.shift = sb(f"ln{n}_shift", [P, NT])
                self.stats_done = sem(f"ln{n}_stats_done")
                self.var_done = sem(f"ln{n}_var_done")
                self.eps_done = sem(f"ln{n}_eps_done")
                self.rstd_done = sem(f"ln{n}_rstd_done")
                self.shift_done = sem(f"ln{n}_shift_done")

        ln1, ln2, ln3, ln4 = Norm(1), Norm(2), Norm(3), Norm(4)
        bias4 = sb("bias4", [P, NT])

        ps_st = [ctx.enter_context(nc.psum_tensor(f"ps_st{i}", [P, S], F32)) for i in range(2)]
        ps_p1 = [ctx.enter_context(nc.psum_tensor(f"ps_p1{i}", [P, S], F32)) for i in range(P1S)]
        ps_pv = ctx.enter_context(nc.psum_tensor("ps_pv", [P, S], F32))
        ps_w = [ctx.enter_context(nc.psum_tensor(f"ps_w{i}", [P, S], F32)) for i in range(2)]

        w_loaded = sem("w_loaded")
        const_zeroed = sem("const_zeroed")
        const_ready = sem("const_ready")
        wo_permuted = sem("wo_permuted")
        w_transposed = sem("w_transposed")
        w_ready = sem("w_ready")
        x_ln_loaded = sem("x_ln_loaded")
        x_res_loaded = sem("x_res_loaded")
        xhat_ready = sem("xhat_ready")
        xT_in_psum = sem("xT_in_psum")
        xT_ready = sem("xT_ready")
        qkv_in_psum = sem("qkv_in_psum")
        hi_ready = sem("hi_ready")
        vT_ready = sem("vT_ready")
        resid_ready = sem("resid_ready")
        mid_ready = sem("mid_ready")
        lo_ready = sem("lo_ready")
        k_stacked = sem("k_stacked")
        q_stacked = sem("q_stacked")
        v_in_psum = sem("v_in_psum")
        v_ready = sem("v_ready")
        p1_in_psum = sem("p1_in_psum")
        p1_reduced = sem("p1_reduced")
        m_hi = sem("m_hi")
        m_res = sem("m_res")
        m_mid = sem("m_mid")
        m_split = sem("m_split")
        mT_in_psum = sem("mT_in_psum")
        mT_ready = sem("mT_ready")
        m_stacked = sem("m_stacked")
        st_in_psum = sem("st_in_psum")
        exp_done = sem("exp_done")
        masked = sem("masked")
        pv_done = sem("pv_done")
        oT_evacuated = sem("oT_evacuated")
        z_gathered = sem("z_gathered")
        o_gathered = sem("o_gathered")
        recip_done = sem("recip_done")
        r_rowed = sem("r_rowed")
        r_spread = sem("r_spread")
        o_normed = sem("o_normed")
        y_in_psum = sem("y_in_psum")
        tsum_ready = sem("tsum_ready")
        x2hat_ready = sem("x2hat_ready")
        x2T_in_psum = sem("x2T_in_psum")
        x2T_ready = sem("x2T_ready")
        f_in_psum = sem("f_in_psum")
        osum_ready = sem("osum_ready")
        bias4_ready = sem("bias4_ready")
        out_ready = sem("out_ready")
        out_stored = [sem("out_stored0"), sem("out_stored1")]

        def over_batches(eng, step, end=B - 2):
            step(0, 0, True, False)
            step(1, 1, True, True)
            with eng.Fori(2, end, 2) as b:
                step(b, 0, True, True)
                step(b + 1, 1, True, True)
            for b in range(end, B):
                step(b, b % 2, b + 1 < B, True)

        def worked_out(eng, count):
            return count if isinstance(count, int) else eng.snap(eng.to_reg(count))

        def p1_at(g, t):
            tiles = [(1, 7), (1, 8), (1, 9)] if t < 3 else [(2, t - 3)]
            ahead, tile = tiles[t] if t < 3 else tiles[0]
            found = [((g + ahead) // KVH, (g + ahead) % KVH, tile)]
            if t == 2:
                found.append(((g + ahead) // KVH, (g + ahead) % KVH, P1 - 1))
            return found

        block = ctx.enter_context(nc.Block())

        @block.sync
        def _(sp):
            sp.dma_start(x_ln[:], x_v[0]).then_inc(x_ln_loaded, 16)
            sp.dma_start(wq_sb[:], wq.rearrange("(c p) i -> p c i", p=P)).then_inc(w_loaded, 16)
            sp.dma_start(wkv_sb[0:64, :], wk).then_inc(w_loaded, 16)
            sp.dma_start(wkv_sb[64:128, :], wv).then_inc(w_loaded, 16)
            sp.dma_start(wo_sb[:], wo.rearrange("(c p) i -> p c i", p=P)).then_inc(w_loaded, 16)
            sp.dma_start(wf_sb[:], wf.rearrange("(c p) i -> p c i", p=P)).then_inc(w_loaded, 16)
            sp.dma_start(dish2[0:R, :], disha).then_inc(w_loaded, 16)
            sp.dma_start(dish2[R:2 * R, :], disha).then_inc(w_loaded, 16)

            def stack_k(d, par):
                sp.wait_ge(lo_ready, 3 * d + 1)
                for n, part in enumerate(K_PART):
                    sp.dma_start(KS[DH * n:DH * (n + 1), par, :, :],
                                 k_split[:, part, :]).then_inc(k_stacked, 16)

            def stack_q(d, par):
                sp.wait_ge(lo_ready, 3 * d + 3)
                for n, part in enumerate(Q_PART):
                    sp.dma_start(QS[DH * n:DH * (n + 1), par, :, :].rearrange("p (s m) t -> p s (m t)", m=2),
                                 q_split[:, part, :, :].rearrange("p m t -> p (m t)")).then_inc(q_stacked, 16)

            def stack_m(n, g, par):
                sp.wait_ge(mT_ready, n + 1)
                sp.dma_start(QS[KR:KM, par, HG * g:HG * (g + 1), :].rearrange("p h (t q) -> p (h t) q", q=P),
                             mT_sb[:, g % 2, :]).then_inc(m_stacked, 16)

            def gather_o(d, par):
                sp.wait_ge(oT_evacuated, 4 * d + 4)
                sp.dma_start(zc[:], OT[DH:P:2 * DH, par, :, :].rearrange("p g t -> p (g t)")).then_inc(z_gathered, 16)
                for c in range(HG):
                    sp.dma_start(oraw[64 * (c % 2):64 * (c % 2) + 64, c // 2, :],
                                 OT[32 * c:32 * c + DH, par, :, :]).then_inc(o_gathered, 16)

            def row_r(d):
                sp.wait_ge(recip_done, d + 1)
                sp.dma_start(r_dram.rearrange("c (k e) -> (c k) e", e=64), rc[:]).then_inc(r_rowed, 16)

            def spread_r(d):
                sp.wait_ge(r_rowed, 16 * (d + 1))
                for c in range(HG):
                    sp.dma_start(rrep[64 * (c % 2):64 * (c % 2) + 64, c // 2, :],
                                 r_dram[c].unsqueeze(0).broadcast_to([DH, KVH * S])).then_inc(r_spread, 16)

            def store_out(d, h):
                sp.wait_ge(out_ready, 2 * d + h + 1)
                sp.dma_start(out_v[d][:, 2 * h:2 * h + 2, :], outb[:, 2 * h:2 * h + 2, :]).then_inc(out_stored[h], 16)

            def load_x_res(d):
                sp.wait_ge(tsum_ready, 2 * d)
                sp.dma_start(x_res[:], x_v[d]).then_inc(x_res_loaded, 16)

            def load_x_ln(d):
                sp.wait_ge(xhat_ready, d)
                sp.dma_start(x_ln[:], x_v[d]).then_inc(x_ln_loaded, 16)

            load_x_ln(1)
            stack_k(0, 0)
            stack_q(0, 0)
            stack_m(0, 0, 0)

            def step(b, par, nxt, prev):
                if prev:
                    load_x_res(b - 1)
                    gather_o(b - 1, 1 - par)
                    row_r(b - 1)
                stack_m(4 * b + 1, 1, par)
                if prev:
                    spread_r(b - 1)
                if nxt:
                    stack_k(b + 1, 1 - par)
                    if not isinstance(b, int) or b + 2 < B:
                        load_x_ln(b + 2)
                    stack_q(b + 1, 1 - par)
                stack_m(4 * b + 2, 2, par)
                stack_m(4 * b + 3, 3, par)
                if nxt:
                    stack_m(4 * b + 4, 0, 1 - par)
                if prev:
                    store_out(b - 1, 0)
                    store_out(b - 1, 1)

            over_batches(sp, step, B - 4)
            load_x_res(B - 1)
            gather_o(B - 1, (B - 1) % 2)
            row_r(B - 1)
            spread_r(B - 1)
            store_out(B - 1, 0)
            store_out(B - 1, 1)
            sp.wait_ge(out_stored[0], 16 * B)
            sp.wait_ge(out_stored[1], 16 * B)

        @block.tensor
        def _(pe):
            def transpose_weights():
                pe.wait_ge(const_ready, 6)
                pe.wait_ge(w_loaded, 16 * 7)
                for c in range(NC):
                    for o in range(2):
                        nc.tensor.transpose(ps_p1[0][:, D * c + P * o:D * c + P * (o + 1)],
                                            wq_sb[:, o, P * c:P * (c + 1)], identf[:])
                for c in range(NC):
                    nc.tensor.transpose(ps_p1[1][:, P * c:P * (c + 1)],
                                        wkv_sb[:, P * c:P * (c + 1)], identf[:]).then_inc(w_transposed, 1)
                pe.wait_ge(wo_permuted, 1)
                for c in range(NC):
                    for o in range(2):
                        nc.tensor.transpose(ps_p1[2][:, D * c + P * o:D * c + P * (o + 1)],
                                            wo_perm[:, o, P * c:P * (c + 1)], identf[:])
                for c in range(NC):
                    for o in range(2):
                        last = nc.tensor.transpose(ps_w[1][:, D * c + P * o:D * c + P * (o + 1)],
                                                   wf_sb[:, o, P * c:P * (c + 1)], identf[:])
                last.then_inc(w_transposed, 1)

            def transpose_x(d, c):
                pe.wait_ge(xhat_ready, d + 1)
                for t in range(NT):
                    last = nc.tensor.transpose(ps_w[c][:, P * t:P * (t + 1)], xhat[:, t, P * c:P * (c + 1)], identf[:])
                last.then_inc(xT_in_psum, 1)

            def project(bank, weights):
                for c in range(NC):
                    last = nc.tensor.matmul(ps_w[bank][:], weights(c), xT[:, c, :], start=(c == 0), stop=(c == NC - 1))
                last.then_inc(qkv_in_psum, 1)

            def project_kv(d):
                pe.wait_ge(xT_ready, 2 * d + 2)
                project(0, lambda c: wkvT[:, c, :])

            def project_q0(d):
                project(1, lambda c: wqT[:, c, 0:P])

            def project_q1(d):
                pe.wait_ge(resid_ready, 3 * d + 1)
                pe.wait_ge(vT_ready, d + 1)
                project(0, lambda c: wqT[:, c, P:2 * P])

            def transpose_v(d):
                v_by, q_by = worked_out(pe, d + 1), worked_out(pe, 3 * d + 2)
                pe.wait_ge(w_ready, 4)
                pe.wait_ge(vT_ready, v_by)
                pe.wait_ge(resid_ready, q_by)
                for t in range(NT):
                    last = nc.tensor.transpose(ps_w[1][:, 64 * t:64 * (t + 1)], vT_sb[64:P, P * t:P * (t + 1)],
                                               identf[64:P, 64:P])
                last.then_inc(v_in_psum, 1)

            def p1_tile(d, g, tile, par):
                at = P1 * g + tile
                per = P1 * KVH
                if tile == 0:
                    if g == 0:
                        pe.wait_ge(k_stacked, 16 * len(K_PART) * (d + 1))
                        pe.wait_ge(q_stacked, 16 * len(Q_PART) * (d + 1))
                if at >= P1S:
                    pe.wait_ge(p1_reduced, per * d + at - P1S + 1)
                elif not (isinstance(d, int) and d == 0):
                    before = max(i for i in range(per) if i % P1S == at)
                    pe.wait_ge(p1_reduced, per * d + before + 1 - per)
                ps = ps_p1[at % P1S]
                if tile < 8:
                    qt, h = 3 - tile // HG, tile % HG
                    heads, n = [h], P * (qt + 1)
                elif tile < 10:
                    qt, heads, n = 1, [2 * (tile - 8), 2 * (tile - 8) + 1], 2 * P
                else:
                    qt, heads, n = 0, list(range(HG)), P
                for i, h in enumerate(heads):
                    nc.tensor.matmul(ps[:, n * i:n * (i + 1)], QS[0:KR, par, HG * g + h, P * qt:P * (qt + 1)],
                                     KS[0:KR, par, g, 0:n], start=(i == 0), stop=False, skip_group_check=True)
                k = len(heads)
                diag = ps[:, 0:n * k].rearrange("p (h k) -> p h k", h=k)[:, :, n - P:n]
                nc.tensor.matmul(diag, identb[:], causal[:].unsqueeze(1).broadcast_to([P, k, P]), start=False,
                                 stop=True, skip_group_check=True).then_inc(p1_in_psum, 1)

            def transpose_m(n, g, bank_left=None):
                split_by = worked_out(pe, n + 1)
                if bank_left:
                    left_by = worked_out(pe, bank_left[1])
                pe.wait_ge(w_ready, 4)
                pe.wait_ge(m_split, split_by)
                if bank_left:
                    pe.wait_ge(bank_left[0], left_by)
                nc.tensor.transpose(ps_w[1][0:3 * H, 0:P // 2].bitcast(BF16), msplit[:].rearrange("p a b -> p (a b)"),
                                    identb[:]).then_inc(mT_in_psum, 1)

            def st_tile(b, g, t, par):
                at = ST * g + t
                if t == 0:
                    pe.wait_ge(m_stacked, 16 * (4 * b + g + 1))
                if not (isinstance(b, int) and b == 0 and at < 2):
                    pe.wait_ge(exp_done, ST * KVH * b + at - 1)
                ps = ps_st[t % 2]
                if t < HG:
                    last = nc.tensor.matmul(ps[:], KS[0:KM, par, g, 0:P], QS[0:KM, par, HG * g + t, :],
                                            start=True, stop=True)
                elif t < 2 * HG:
                    h = HG * g + t - HG
                    nc.tensor.matmul(ps[:, P:S], KS[0:KM, par, g, P:2 * P], QS[0:KM, par, h, P:S],
                                     start=True, stop=True)
                    last = nc.tensor.matmul(ps[:, 0:P], KS[0:KM, par, g, 3 * P:S], QS[0:KM, par, h, 3 * P:S],
                                            start=True, stop=True)
                else:
                    h = HG * g + 2 * (t - 2 * HG)
                    last = nc.tensor.matmul(ps[:].rearrange("p (h q) -> p h q", h=2), KS[0:KM, par, g, 2 * P:3 * P],
                                            QS[0:KM, par, h:h + 2, 2 * P:S], start=True, stop=True)
                last.then_inc(st_in_psum, 1)

            def pv(n, g, par, kt):
                tile = {0: 0, 1: HG, 3: HG, 2: 2 * HG}[kt]
                pe.wait_ge(masked, 3 * n + {0: 1, 1: 2, 3: 2, 2: 3}[kt])
                if kt == 0:
                    if not (isinstance(n, int) and n == 0):
                        pe.wait_ge(oT_evacuated, n)
                for h in range(HG):
                    slot = ST * (g % 2) + tile + (h // 2 if kt == 2 else h)
                    lo = {0: 0, 1: P, 3: 0, 2: 2 * P * (h % 2)}[kt]
                    width = S - P * kt
                    last = nc.tensor.matmul(ps_pv[32 * h:32 * (h + 1), P * kt:S], V1[:, par, kt, g, :],
                                            PT[:, slot, lo:lo + width], start=(kt == 0), stop=(kt == 2),
                                            tile_position=(0, 32 * h), skip_group_check=True)
                if kt == 2:
                    last.then_inc(pv_done, 1)

            def out_project(d, h):
                if h == 0:
                    pe.wait_ge(o_normed, 2 * d + 2)
                for t in range(2):
                    for c in range(NC):
                        last = nc.tensor.matmul(ps_w[h][:, D * t:D * (t + 1)],
                                                oT[:, c, P * (2 * h + t):P * (2 * h + t + 1)], woT[:, c, :],
                                                start=(c == 0), stop=(c == NC - 1), skip_group_check=True)
                last.then_inc(y_in_psum, 1)

            def transpose_x2(d, c):
                pe.wait_ge(x2hat_ready, 2 * d + 2)
                for t in range(NT):
                    last = nc.tensor.transpose(ps_w[c][:, P * t:P * (t + 1)], x2hat[:, t, P * c:P * (c + 1)], identf[:])
                last.then_inc(x2T_in_psum, 1)

            def ffn(d, h):
                if h == 0:
                    pe.wait_ge(x2T_ready, 2 * d + 2)
                for t in range(2):
                    for c in range(NC):
                        last = nc.tensor.matmul(ps_w[h][:, D * t:D * (t + 1)],
                                                x2T[:, c, P * (2 * h + t):P * (2 * h + t + 1)], wfT[:, c, :],
                                                start=(c == 0), stop=(c == NC - 1), skip_group_check=True)
                last.then_inc(f_in_psum, 1)

            transpose_weights()
            pe.wait_ge(w_ready, 4)
            for c in range(NC):
                transpose_x(0, c)
            project_kv(0)
            project_q0(0)
            project_q1(0)
            transpose_v(0)
            for tile in range(P1):
                p1_tile(0, 0, tile, 0)
            transpose_m(0, 0, (v_ready, 1))
            for tile in range(7):
                p1_tile(0, 1, tile, 0)

            def step(b, par, nxt, prev):
                n0 = 4 * b
                first = isinstance(b, int) and b == 0
                for g in range(KVH):
                    n = n0 + g
                    for t in range(ST):
                        st_tile(b, g, t, par)
                        for ahead, pg, tile in p1_at(g, t):
                            if ahead == 0 or nxt:
                                p1_tile(b + ahead, pg, tile, par if ahead == 0 else 1 - par)
                        if not (first and g == 0):
                            if t == 1:
                                pv(n - 1, (g - 1) % KVH, par if g else 1 - par, 1)
                                pv(n - 1, (g - 1) % KVH, par if g else 1 - par, 3)
                            if t == 2:
                                pv(n - 1, (g - 1) % KVH, par if g else 1 - par, 2)
                        if t == 6 and (g < 3 or nxt):
                            bank_left = None
                            if g == 0 and prev:
                                bank_left = osum_ready, 2 * b
                            if g == 1 and nxt:
                                bank_left = v_ready, b + 2
                            if g == 2 and prev:
                                bank_left = tsum_ready, 2 * b
                            if g == 3 and prev:
                                bank_left = x2T_ready, 2 * b
                            transpose_m(n + 1, (g + 1) % KVH, bank_left)
                        if t == 7:
                            pv(n, g, par, 0)
                        if nxt:
                            if (g, t) == (0, 5):
                                if prev:
                                    pe.wait_ge(osum_ready, 2 * b - 1)
                                transpose_x(b + 1, 0)
                            if (g, t) == (0, 7):
                                pe.wait_ge(mT_ready, n0 + 2)
                                transpose_x(b + 1, 1)
                            if (g, t) == (0, 8):
                                project_kv(b + 1)
                            if (g, t) == (0, 9):
                                project_q0(b + 1)
                            if (g, t) == (1, 1):
                                project_q1(b + 1)
                            if (g, t) == (1, 4):
                                transpose_v(b + 1)
                        if prev:
                            if (g, t) == (1, 8):
                                if nxt:
                                    pe.wait_ge(resid_ready, 3 * (b + 1) + 3)
                                else:
                                    pe.wait_ge(osum_ready, 2 * b - 1)
                                out_project(b - 1, 0)
                            if (g, t) == (1, 9):
                                pe.wait_ge(mT_ready, n0 + 3)
                                out_project(b - 1, 1)
                            if (g, t) == (2, 8):
                                transpose_x2(b - 1, 0)
                            if (g, t) == (2, 9):
                                pe.wait_ge(mT_ready, n0 + 4)
                                transpose_x2(b - 1, 1)
                            if (g, t) == (3, 3):
                                ffn(b - 1, 0)
                            if (g, t) == (3, 7):
                                if nxt:
                                    pe.wait_ge(mT_ready, n0 + 5)
                                ffn(b - 1, 1)

            over_batches(pe, step)
            last_g, last_par = KVH - 1, (B - 1) % 2
            for kt in (1, 3, 2):
                pv(KVH * B - 1, last_g, last_par, kt)
            pe.wait_ge(osum_ready, 2 * (B - 1) + 2)
            out_project(B - 1, 0)
            out_project(B - 1, 1)
            transpose_x2(B - 1, 0)
            transpose_x2(B - 1, 1)
            ffn(B - 1, 0)
            ffn(B - 1, 1)

        @block.scalar
        def _(act):
            def copy_xT(d, c):
                act.wait_ge(xT_in_psum, 2 * d + c + 1)
                nc.scalar.copy(xT[:, c, :], ps_w[c][:]).then_inc(xT_ready, 1)

            def split_hi_k(d):
                act.wait_ge(qkv_in_psum, 3 * d + 1)
                if not (isinstance(d, int) and d == 0):
                    act.wait_ge(k_stacked, 16 * len(K_PART) * d)
                nc.scalar.copy(k_split[:, HI, :], ps_w[0][0:64, :]).then_inc(hi_ready, 1)
                nc.scalar.copy(vT_sb[64:P, :], ps_w[0][64:P, :]).then_inc(vT_ready, 1)

            def split_hi_q(d, half):
                act.wait_ge(qkv_in_psum, 3 * d + 2 + half)
                if not (isinstance(d, int) and d == 0):
                    act.wait_ge(q_stacked, 16 * len(Q_PART) * d)
                nc.scalar.mul(q_split[:, HI, half, :], ps_w[1 - half][:], SCALE).then_inc(hi_ready, 1)

            def copy_v(d, par):
                act.wait_ge(v_in_psum, d + 1)
                nc.scalar.copy(V1[:, par, :, :, 0:DH],
                               ps_w[1][:, 0:D].rearrange("p (t g d) -> p t g d", t=NT, d=DH)).then_inc(v_ready, 1)

            def copy_mT(n, g):
                act.wait_ge(mT_in_psum, n + 1)
                if not (isinstance(n, int) and n < 2):
                    act.wait_ge(m_stacked, 16 * (n - 1))
                nc.scalar.copy(mT_sb[:, g % 2, :], ps_w[1][0:3 * H, 0:P // 2].bitcast(BF16)).then_inc(mT_ready, 1)

            def exp_tile(b, g, t):
                act.wait_ge(st_in_psum, ST * (KVH * b + g) + t + 1)
                if t == 0 and not (isinstance(b, int) and b == 0 and g < 2):
                    act.wait_ge(pv_done, 4 * b + g - 1)
                nc.scalar.activation(PT[:, ST * (g % 2) + t, :], ps_st[t % 2][:], ACT.Exp).then_inc(exp_done, 1)

            def copy_oT(n, g, par, d):
                act.wait_ge(pv_done, n + 1)
                if g == 0 and not (isinstance(d, int) and d < 2):
                    act.wait_ge(z_gathered, 16 * (d - 1))
                    act.wait_ge(o_gathered, 64 * (d - 1))
                nc.scalar.copy(OT[:, par, g, :], ps_pv[:]).then_inc(oT_evacuated, 1)

            def apply_ln3(d, h):
                act.wait_ge(ln3.shift_done, 2 * d + h + 1)
                for t in (2 * h, 2 * h + 1):
                    last = nc.scalar.activation(x2hat[:, t, :], tsum[:, t, :], ACT.Identity,
                                                bias=ln3.shift[:, t:t + 1], scale=ln3.rstd[:, t:t + 1])
                last.then_inc(x2hat_ready, 1)

            def copy_x2T(d, c):
                act.wait_ge(x2T_in_psum, 2 * d + c + 1)
                nc.scalar.copy(x2T[:, c, :], ps_w[c][:]).then_inc(x2T_ready, 1)

            def finish_out(d, h):
                act.wait_ge(bias4_ready, 2 * d + h + 1)
                if not (isinstance(d, int) and d == 0):
                    act.wait_ge(out_stored[h], 16 * d)
                for t in (2 * h, 2 * h + 1):
                    last = nc.scalar.activation(outb[:, t, :], osum[:, t, :], ACT.Identity, bias=bias4[:, t:t + 1])
                last.then_inc(out_ready, 1)

            act.wait_ge(w_ready, 4)
            copy_xT(0, 0)
            copy_xT(0, 1)
            split_hi_k(0)
            split_hi_q(0, 0)
            split_hi_q(0, 1)
            copy_v(0, 0)
            copy_mT(0, 0)

            def step(b, par, nxt, prev):
                n0 = 4 * b
                first = isinstance(b, int) and b == 0
                for g in range(KVH):
                    for t in range(ST):
                        exp_tile(b, g, t)
                        if t == 3 and not (first and g == 0):
                            copy_oT(n0 + g - 1, (g - 1) % KVH, par if g else 1 - par, b if g else b - 1)
                        if t == 7 and (g < 3 or nxt):
                            copy_mT(n0 + g + 1, (g + 1) % KVH)
                        if nxt:
                            if (g, t) == (0, 6):
                                copy_xT(b + 1, 0)
                            if (g, t) == (0, 7):
                                copy_xT(b + 1, 1)
                            if (g, t) == (0, 9):
                                split_hi_k(b + 1)
                            if (g, t) == (1, 0):
                                split_hi_q(b + 1, 0)
                            if (g, t) == (1, 2):
                                split_hi_q(b + 1, 1)
                            if (g, t) == (1, 5):
                                copy_v(b + 1, 1 - par)
                        if prev:
                            if (g, t) == (2, 5):
                                apply_ln3(b - 1, 0)
                            if (g, t) == (2, 7):
                                apply_ln3(b - 1, 1)
                            if (g, t) == (2, 9):
                                copy_x2T(b - 1, 0)
                            if (g, t) == (3, 0):
                                copy_x2T(b - 1, 1)
                            if (g, t) == (3, 8):
                                finish_out(b - 1, 0)
                            if (g, t) == (3, 9):
                                finish_out(b - 1, 1)

            over_batches(act, step)
            copy_oT(KVH * B - 1, KVH - 1, (B - 1) % 2, B - 1)
            apply_ln3(B - 1, 0)
            apply_ln3(B - 1, 1)
            copy_x2T(B - 1, 0)
            copy_x2T(B - 1, 1)
            finish_out(B - 1, 0)
            finish_out(B - 1, 1)

        @block.vector
        def _(dve):
            def constants():
                nc.vector.memset(powexp[:], -0.5).then_inc(const_ready, 1)
                nc.vector.memset(KS[KR:KM], 1.0).then_inc(const_ready, 1)
                nc.vector.memset(V1[:, :, :, :, DH:2 * DH], 1.0).then_inc(const_ready, 1)

            def permute_wo():
                dve.wait_ge(w_loaded, 16 * 7)
                for o in range(2):
                    for cc in range(NC):
                        src = wo_sb[:, o, :].rearrange("p (g c d) -> p c d g", g=KVH, c=HG)[:, 2 * cc:2 * cc + 2, :, :]
                        dst = wo_perm[:, o, P * cc:P * (cc + 1)].rearrange("p (c d g) -> p c d g", c=2, d=DH)
                        last = nc.vector.tensor_copy(dst, src)
                last.then_inc(wo_permuted, 1)

            def lay_out_weights():
                dve.wait_ge(w_transposed, 2)
                for c in range(NC):
                    nc.vector.tensor_copy(
                        wqT[:, c, :].rearrange("p (m d s) -> p m d s", m=2, d=DH),
                        ps_p1[0][:, D * c:D * (c + 1)].rearrange("p (s m d) -> p m d s", s=8, m=2))
                dve.wait_ge(w_transposed, 2)
                for c in range(NC):
                    nc.vector.tensor_copy(wkvT[:, c, 0:64].rearrange("p (d g) -> p d g", d=DH),
                                          ps_p1[1][:, P * c:P * c + 64].rearrange("p (g d) -> p d g", g=KVH))
                    last = nc.vector.tensor_copy(wkvT[:, c, 64:P], ps_p1[1][:, P * c + 64:P * (c + 1)])
                last.then_inc(w_ready, 2)
                dve.wait_ge(w_transposed, 3)
                nc.vector.tensor_copy(woT[:].rearrange("p c o -> p (c o)"), ps_p1[2][:]).then_inc(w_ready, 1)
                nc.vector.tensor_tensor(wfT[:], ps_w[1][:].rearrange("p (c o) -> p c o", c=NC),
                                        dish2[:].unsqueeze(1).broadcast_to([P, NC, D]), ALU.add).then_inc(w_ready, 1)

            def stats(ln, src, tiles, done):
                for t in tiles:
                    last = nc.vector.bn_stats(ln.stats[:, t, :], src(t))
                last.then_inc(ln.stats_done, 1)

            def aggregate(ln, tiles, done):
                done_by = worked_out(dve, done + 1)
                dve.wait_ge(w_loaded, 16 * 7)
                dve.wait_ge(ln.stats_done, done_by)
                for t in tiles:
                    last = nc.vector.bn_aggr(ln.mv[:, t, :], ln.stats[:, t, :])
                last.then_inc(ln.var_done, 1)

            def shift(ln, h, done):
                a, b = 2 * h, 2 * h + 2
                dve.wait_ge(ln.rstd_done, done + 1)
                nc.vector.scalar_tensor_tensor(ln.shift[:, a:b], ln.mv[:, a:b, 0], -1.0, ln.rstd[:, a:b],
                                               ALU.mult, ALU.mult).then_inc(ln.shift_done, 1)

            def ln1_stats(d):
                dve.wait_ge(x_ln_loaded, 16 * (d + 1))
                stats(ln1, lambda t: x_ln[:, t, :], range(NT), d)
                aggregate(ln1, range(NT), d)

            def ln1_apply(d):
                dve.wait_ge(ln1.rstd_done, d + 1)
                if not (isinstance(d, int) and d == 0):
                    dve.wait_ge(xT_in_psum, 2 * d)
                for t in range(NT):
                    last = nc.vector.tensor_scalar(xhat[:, t, :], x_ln[:, t, :], ln1.mv[:, t, 0:1],
                                                   ln1.rstd[:, t:t + 1], ALU.subtract, ALU.mult)
                last.then_inc(xhat_ready, 1)

            def split_rest(d, i):
                dve.wait_ge(hi_ready, 3 * d + i + 1)
                if i == 0:
                    rows, ps, scale, part = 64, ps_w[0], 1.0, lambda p: k_split[:, p, :]
                else:
                    rows, ps, scale = P, ps_w[2 - i], SCALE
                    part = lambda p: q_split[:, p, i - 1, :]
                if not (isinstance(d, int) and d == 0):
                    dve.wait_ge(lo_ready, 3 * d + i - 2)
                nc.vector.scalar_tensor_tensor(resid[0:rows, i, :], ps[0:rows, :], scale, part(HI),
                                               ALU.mult, ALU.subtract).then_inc(resid_ready, 1)
                dve.wait_ge(resid_ready, 3 * d + i + 1)
                nc.vector.tensor_copy(part(MID), resid[0:rows, i, :]).then_inc(mid_ready, 1)

            def p1_reduce(d, g, tile):
                at = P1 * g + tile
                n = 4 * d + g
                if tile == 0 and not (isinstance(d, int) and d == 0 and g < 2):
                    dve.wait_ge(m_split, n - 1)
                dve.wait_ge(p1_in_psum, P1 * n + tile + 1)
                ps = ps_p1[at % P1S]
                if tile < 8:
                    qt, h0, k = 3 - tile // HG, tile % HG, 1
                elif tile < 10:
                    qt, h0, k = 1, 2 * (tile - 8), 2
                else:
                    qt, h0, k = 0, 0, HG
                w = P * (qt + 1)
                m = mneg[:, g % 2, :].rearrange("p (h t) -> p h t", h=HG)[:, h0:h0 + k, qt]
                nc.vector.tensor_reduce(m, ps[:, 0:w * k].rearrange("p (h k) -> p h k", h=k), AX.X, ALU.max,
                                        negate=True).then_inc(p1_reduced, 1)

            def recip(d):
                dve.wait_ge(z_gathered, 16 * (d + 1))
                if not (isinstance(d, int) and d == 0):
                    dve.wait_ge(r_rowed, 16 * d)
                nc.vector.reciprocal(rc[:], zc[:]).then_inc(recip_done, 1)

            def ln2_stats(d, h):
                dve.wait_ge(y_in_psum, 2 * d + h + 1)
                stats(ln2, lambda t: ps_w[h][:, D * (t % 2):D * (t % 2 + 1)], (2 * h, 2 * h + 1), 2 * d + h)
                aggregate(ln2, (2 * h, 2 * h + 1), 2 * d + h)

            def ln2_apply(d, h):
                if h == 0:
                    dve.wait_ge(x_res_loaded, 16 * (d + 1))
                    if not (isinstance(d, int) and d == 0):
                        dve.wait_ge(x2hat_ready, 2 * d)
                dve.wait_ge(ln2.rstd_done, 2 * d + h + 1)
                for t in (2 * h, 2 * h + 1):
                    last = nc.vector.scalar_tensor_tensor(tsum[:, t, :], ps_w[h][:, D * (t % 2):D * (t % 2 + 1)],
                                                          ln2.rstd[:, t:t + 1], x_res[:, t, :], ALU.mult, ALU.add)
                last.then_inc(tsum_ready, 1)
                shift(ln2, h, 2 * d + h)

            def ln3_stats(d, h):
                dve.wait_ge(tsum_ready, 2 * d + h + 1)
                stats(ln3, lambda t: tsum[:, t, :], (2 * h, 2 * h + 1), 2 * d + h)
                aggregate(ln3, (2 * h, 2 * h + 1), 2 * d + h)

            def ln4_stats(d, h):
                dve.wait_ge(f_in_psum, 2 * d + h + 1)
                stats(ln4, lambda t: ps_w[h][:, D * (t % 2):D * (t % 2 + 1)], (2 * h, 2 * h + 1), 2 * d + h)
                aggregate(ln4, (2 * h, 2 * h + 1), 2 * d + h)

            def ln4_apply(d, h):
                a, b = 2 * h, 2 * h + 2
                dve.wait_ge(ln4.rstd_done, 2 * d + h + 1)
                if not (isinstance(d, int) and d == 0):
                    dve.wait_ge(out_ready, 2 * d)
                for t in range(a, b):
                    last = nc.vector.scalar_tensor_tensor(osum[:, t, :], ps_w[h][:, D * (t % 2):D * (t % 2 + 1)],
                                                          ln4.rstd[:, t:t + 1], tsum[:, t, :], ALU.mult, ALU.add)
                last.then_inc(osum_ready, 1)
                shift(ln4, h, 2 * d + h)
                dve.wait_ge(ln4.shift_done, 2 * d + h + 1)
                dve.wait_ge(osum_ready, 2 * d + h + 3)
                nc.vector.tensor_tensor(bias4[:, a:b], ln4.shift[:, a:b], ln2.shift[:, a:b],
                                        ALU.add).then_inc(bias4_ready, 1)

            dve.sem_inc(osum_ready, 2)
            constants()
            permute_wo()
            ln1_stats(0)
            ln1_apply(0)
            lay_out_weights()
            for i in range(3):
                split_rest(0, i)
            for tile in range(P1):
                p1_reduce(0, 0, tile)
            for tile in range(7):
                p1_reduce(0, 1, tile)

            def step(b, par, nxt, prev):
                for g in range(KVH):
                    for t in range(ST):
                        for ahead, pg, tile in p1_at(g, t):
                            if ahead == 0 or nxt:
                                p1_reduce(b + ahead, pg, tile)
                        if nxt:
                            if (g, t) == (0, 0):
                                ln1_stats(b + 1)
                            if (g, t) == (0, 3):
                                ln1_apply(b + 1)
                            if (g, t) == (1, 0):
                                split_rest(b + 1, 0)
                            if (g, t) == (1, 1):
                                split_rest(b + 1, 1)
                            if (g, t) == (1, 3):
                                split_rest(b + 1, 2)
                        if prev:
                            if (g, t) == (0, 7):
                                recip(b - 1)
                            if (g, t) == (1, 9):
                                ln2_stats(b - 1, 0)
                            if (g, t) == (2, 0):
                                ln2_stats(b - 1, 1)
                            if (g, t) == (2, 1):
                                ln2_apply(b - 1, 0)
                                ln3_stats(b - 1, 0)
                            if (g, t) == (2, 3):
                                ln2_apply(b - 1, 1)
                                ln3_stats(b - 1, 1)
                            if (g, t) == (2, 4):
                                shift(ln3, 0, 2 * (b - 1))
                            if (g, t) == (2, 6):
                                shift(ln3, 1, 2 * (b - 1) + 1)
                            if (g, t) == (3, 4):
                                ln4_stats(b - 1, 0)
                            if (g, t) == (3, 6):
                                ln4_apply(b - 1, 0)
                            if (g, t) == (3, 8):
                                ln4_stats(b - 1, 1)
                            if (g, t) == (3, 9):
                                ln4_apply(b - 1, 1)

            over_batches(dve, step)
            recip(B - 1)
            for h in range(2):
                ln2_stats(B - 1, h)
            for h in range(2):
                ln2_apply(B - 1, h)
                ln3_stats(B - 1, h)
            for h in range(2):
                shift(ln3, h, 2 * (B - 1) + h)
            for h in range(2):
                ln4_stats(B - 1, h)
            for h in range(2):
                ln4_apply(B - 1, h)

        @block.gpsimd
        def _(pool):
            def constants():
                nc.gpsimd.memset(identf[:], 0.0).then_inc(const_zeroed, 1)
                nc.gpsimd.memset(identb[:], 0.0).then_inc(const_zeroed, 1)
                nc.gpsimd.memset(causal[:], 0.0).then_inc(const_zeroed, 1)
                pool.wait_ge(const_zeroed, 3)
                for m in (identf, identb):
                    nc.gpsimd.affine_select(out=m[:], in_=m[:], compare_op=ALU.not_equal, fill=1.0, base=0,
                                            pattern=[[-1, P]], channel_multiplier=1).then_inc(const_ready, 1)
                nc.gpsimd.affine_select(out=causal[:], in_=causal[:], compare_op=ALU.is_ge, fill=NEG, base=0,
                                        pattern=[[-1, P]], channel_multiplier=1).then_inc(const_ready, 1)

            def rstd(ln, tiles, done):
                a, b = tiles
                done_by = worked_out(pool, done + 1)
                pool.wait_ge(const_ready, 6)
                pool.wait_ge(ln.var_done, done_by)
                nc.gpsimd.tensor_scalar(ln.veps[:, a:b], ln.mv[:, a:b, 1], EPS, None,
                                        ALU.add).then_inc(ln.eps_done, 1)
                pool.wait_ge(ln.eps_done, done + 1)
                nc.gpsimd.tensor_tensor(ln.rstd[:, a:b], ln.veps[:, a:b], powexp[:, a:b],
                                        ALU.pow).then_inc(ln.rstd_done, 1)

            def split_lo(d, i):
                pool.wait_ge(mid_ready, 3 * d + i + 1)
                rows = 64 if i == 0 else P
                part = (lambda p: k_split[:, p, :]) if i == 0 else (lambda p: q_split[:, p, i - 1, :])
                nc.gpsimd.tensor_tensor(part(LO), resid[0:rows, i, :], part(MID), ALU.subtract).then_inc(lo_ready, 1)

            def split_max(n, g):
                maxima_by, parts_by = worked_out(pool, P1 * (n + 1)), worked_out(pool, n)
                pool.wait_ge(const_ready, 6)
                pool.wait_ge(p1_reduced, maxima_by)
                if not (isinstance(n, int) and n == 0):
                    pool.wait_ge(mT_in_psum, parts_by)
                m = mneg[:, g % 2, :]
                nc.gpsimd.tensor_copy(msplit[:, HI, :], m).then_inc(m_hi, 1)
                pool.wait_ge(m_hi, n + 1)
                nc.gpsimd.tensor_tensor(mres[:], m, msplit[:, HI, :], ALU.subtract).then_inc(m_res, 1)
                done_by = worked_out(pool, n + 1)
                pool.wait_ge(const_ready, 6)
                pool.wait_ge(m_res, done_by)
                nc.gpsimd.tensor_copy(msplit[:, MID, :], mres[:]).then_inc(m_mid, 1)
                pool.wait_ge(m_mid, n + 1)
                nc.gpsimd.tensor_tensor(msplit[:, LO, :], mres[:], msplit[:, MID, :], ALU.subtract).then_inc(m_split, 1)

            def mask(n, g, kind):
                s0 = ST * (g % 2)
                first, count = [(0, HG), (HG, HG), (2 * HG, 2)][kind]
                done_by = worked_out(pool, ST * n + first + count)
                pool.wait_ge(const_ready, 6)
                pool.wait_ge(exp_done, done_by)
                v = PT[:, s0 + first:s0 + first + count, :]
                if kind == 0:
                    v, blocks = v[:, :, 0:P], HG
                elif kind == 1:
                    v, blocks = v[:, :, 0:2 * P], 2 * HG
                else:
                    v, blocks = v.rearrange("p s (a q) -> p (s a) q", a=2)[:, :, 0:P], HG
                nc.gpsimd.affine_select(out=v, in_=v, compare_op=ALU.is_ge, fill=0.0, base=0,
                                        pattern=[[0, blocks], [1, P]],
                                        channel_multiplier=-1).then_inc(masked, 1)

            def norm_o(d, par):
                pool.wait_ge(r_spread, 64 * (d + 1))
                pool.wait_ge(o_gathered, 64 * (d + 1))
                if not (isinstance(d, int) and d == 0):
                    pool.wait_ge(y_in_psum, 2 * d)
                for c in range(NC):
                    nc.gpsimd.tensor_tensor(oT[:, c, :], oraw[:, c, :], rrep[:, c, :],
                                            ALU.mult).then_inc(o_normed, 1)

            constants()
            rstd(ln1, (0, NT), 0)
            for i in range(3):
                split_lo(0, i)
            split_max(0, 0)

            def step(b, par, nxt, prev):
                n0 = 4 * b
                for g in range(KVH):
                    n = n0 + g
                    if g == 0 and nxt:
                        rstd(ln1, (0, NT), b + 1)
                    if g == 1 and nxt:
                        split_lo(b + 1, 0)
                        split_lo(b + 1, 1)
                    if g == 2 and prev:
                        rstd(ln2, (0, 2), 2 * (b - 1))
                        rstd(ln2, (2, 4), 2 * (b - 1) + 1)
                        rstd(ln3, (0, 2), 2 * (b - 1))
                    if g < 3 or nxt:
                        split_max(n + 1, (g + 1) % KVH)
                    mask(n, g, 0)
                    if g == 1 and nxt:
                        split_lo(b + 1, 2)
                    if g == 2 and prev:
                        rstd(ln3, (2, 4), 2 * (b - 1) + 1)
                    if g == 3 and prev:
                        rstd(ln4, (0, 2), 2 * (b - 1))
                    if g == 1 and prev:
                        norm_o(b - 1, 1 - par)
                    mask(n, g, 1)
                    mask(n, g, 2)
                    if g == 3 and prev:
                        rstd(ln4, (2, 4), 2 * (b - 1) + 1)

            over_batches(pool, step)
            norm_o(B - 1, (B - 1) % 2)
            for h in range(2):
                rstd(ln2, (2 * h, 2 * h + 2), 2 * (B - 1) + h)
            for h in range(2):
                rstd(ln3, (2 * h, 2 * h + 2), 2 * (B - 1) + h)
            for h in range(2):
                rstd(ln4, (2 * h, 2 * h + 2), 2 * (B - 1) + h)


_INS = ["L0_attn_x", "L0_attn_Wq", "L0_attn_Wk", "L0_attn_Wv", "L0_attn_Wo", "L0_ffn_weight", "L0_ffn_disha"]


def kernel(**inputs):
    import numpy as np
    import concourse.bacc as bacc
    from concourse.bass_utils import run_bass_kernel_spmd

    nc = bacc.Bacc("TRN2", target_bir_lowering=False, num_devices=1)
    arrays, args = {}, []
    for name in _INS:
        a = np.ascontiguousarray(inputs[name])
        arrays[name] = a
        args.append(nc.dram_tensor(name, a.shape, mybir.dt.from_np(a.dtype), kind="ExternalInput").ap())
    shape = inputs["L0_attn_x"].shape
    out = nc.dram_tensor("block_out", shape, mybir.dt.float32, kind="ExternalOutput").ap()
    sandwich_kernel(nc, *args, out)
    return run_bass_kernel_spmd(nc, [arrays], core_ids=[0]).results[0]["block_out"]
```

```python
import concourse.bass as bass
from concourse import mybir
from contextlib import ExitStack


def sandwich_kernel(nc, x, wq, wk, wv, wo, wf, disha, out):
    F32, BF16 = mybir.dt.float32, mybir.dt.bfloat16
    ALU = mybir.AluOpType
    ACT = mybir.ActivationFunctionType
    AX = mybir.AxisListType

    B, S, D = x.shape
    H, DH, P = 16, 16, 128
    KVH = wk.shape[0] // DH
    HG = H // KVH
    R = disha.shape[0]
    NT = S // P
    NC = D // P
    SCALE = DH ** -0.5
    EPS = 1e-5
    NEG = -3.0e38
    HI, MID, LO = 0, 1, 2
    Q_PART = [HI, HI, MID, HI, MID, LO]
    K_PART = [HI, MID, HI, LO, MID, HI]
    KR = len(Q_PART) * DH
    KM = KR + 3
    ST = 10
    P1 = 11
    P1S = 3

    x_v = x.rearrange("b (t p) f -> b p t f", p=P)
    out_v = out.rearrange("b (t p) f -> b p t f", p=P)

    ctx = ExitStack()
    with ctx:
        def sb(name, shape, dt=F32):
            return ctx.enter_context(nc.sbuf_tensor(name, shape, dt))

        def sem(name):
            return ctx.enter_context(nc.semaphore(name))

        wq_sb = sb("wq_sb", [P, 2, D])
        wkv_sb = sb("wkv_sb", [P, D])
        wo_sb = sb("wo_sb", [P, 2, D])
        wo_perm = sb("wo_perm", [P, 2, D])
        wf_sb = sb("wf_sb", [P, 2, D])
        dish2 = sb("dish2", [P, D])
        wqT = sb("wqT", [P, NC, D])
        wkvT = sb("wkvT", [P, NC, P])
        woT = sb("woT", [P, NC, D])
        wfT = sb("wfT", [P, NC, D])
        identf = sb("identf", [P, P])
        identb = sb("identb", [P, P], BF16)
        causal = sb("causal", [P, P], BF16)
        powexp = sb("powexp", [P, NT])

        x_ln = sb("x_ln", [P, NT, D])
        xhat = sb("xhat", [P, NT, D])
        xT = sb("xT", [P, NC, S])
        q_split = sb("q_split", [P, 3, 2, S], BF16)
        k_split = sb("k_split", [64, 3, S], BF16)
        resid = sb("resid", [P, 3, S])
        kvT_sb = sb("kvT_sb", [P, S])
        QS = sb("QS", [P, 2, H, S], BF16)
        KS = sb("KS", [P, 2, KVH, S], BF16)
        V1 = sb("V1", [P, 2, NT, KVH, 2 * DH])

        mneg = sb("mneg", [P, 2, H])
        mres = sb("mres", [P, H])
        msplit = sb("msplit", [P, P // H, H], BF16)
        mT_sb = sb("mT_sb", [3 * H, 2, P], BF16)
        PT = sb("PT", [P, 2 * ST, S])
        OT = sb("OT", [P, 2, KVH, S])

        zc = sb("zc", [P, 64])
        rc = sb("rc", [P, 64])
        r_dram = nc.dram_tensor("r_scratch", (HG, KVH * S), F32, kind="Internal").ap()
        rrep = sb("rrep", [P, NC, S])
        oraw = sb("oraw", [P, NC, S])
        oT = sb("oT", [P, NC, S])
        x_res = sb("x_res", [P, NT, D])
        tsum = sb("tsum", [P, NT, D])
        x2hat = sb("x2hat", [P, NT, D])
        x2T = sb("x2T", [P, NC, S])
        osum = sb("osum", [P, NT, D])
        outb = sb("outb", [P, NT, D])

        class Norm:
            def __init__(self, n):
                self.stats = sb(f"ln{n}_stats", [P, NT, 6])
                self.mv = sb(f"ln{n}_mv", [P, NT, 2])
                self.veps = sb(f"ln{n}_veps", [P, NT])
                self.rstd = sb(f"ln{n}_rstd", [P, NT])
                self.shift = sb(f"ln{n}_shift", [P, NT])
                self.stats_done = sem(f"ln{n}_stats_done")
                self.var_done = sem(f"ln{n}_var_done")
                self.eps_done = sem(f"ln{n}_eps_done")
                self.rstd_done = sem(f"ln{n}_rstd_done")
                self.shift_done = sem(f"ln{n}_shift_done")

        ln1, ln2, ln3, ln4 = Norm(1), Norm(2), Norm(3), Norm(4)
        bias4 = sb("bias4", [P, NT])

        ps_st = [ctx.enter_context(nc.psum_tensor(f"ps_st{i}", [P, S], F32)) for i in range(2)]
        ps_p1 = [ctx.enter_context(nc.psum_tensor(f"ps_p1{i}", [P, S], F32)) for i in range(P1S)]
        ps_pv = ctx.enter_context(nc.psum_tensor("ps_pv", [P, S], F32))
        ps_w = [ctx.enter_context(nc.psum_tensor(f"ps_w{i}", [P, S], F32)) for i in range(2)]

        w_loaded = sem("w_loaded")
        const_zeroed = sem("const_zeroed")
        const_ready = sem("const_ready")
        wo_permuted = sem("wo_permuted")
        w_transposed = sem("w_transposed")
        w_ready = sem("w_ready")
        x_ln_loaded = sem("x_ln_loaded")
        x_res_loaded = sem("x_res_loaded")
        xhat_ready = sem("xhat_ready")
        xT_in_psum = sem("xT_in_psum")
        xT_ready = sem("xT_ready")
        qkv_in_psum = sem("qkv_in_psum")
        hi_ready = sem("hi_ready")
        kvT_ready = sem("kvT_ready")
        resid_ready = sem("resid_ready")
        mid_ready = sem("mid_ready")
        lo_ready = sem("lo_ready")
        k_stacked = sem("k_stacked")
        q_stacked = sem("q_stacked")
        v_in_psum = sem("v_in_psum")
        v_ready = sem("v_ready")
        p1_in_psum = sem("p1_in_psum")
        p1_reduced = sem("p1_reduced")
        m_hi = sem("m_hi")
        m_res = sem("m_res")
        m_mid = sem("m_mid")
        m_split = sem("m_split")
        mT_in_psum = sem("mT_in_psum")
        mT_ready = sem("mT_ready")
        m_stacked = sem("m_stacked")
        st_in_psum = sem("st_in_psum")
        exp_done = sem("exp_done")
        masked = sem("masked")
        pv_done = sem("pv_done")
        oT_evacuated = sem("oT_evacuated")
        z_gathered = sem("z_gathered")
        o_gathered = sem("o_gathered")
        recip_done = sem("recip_done")
        r_rowed = sem("r_rowed")
        r_spread = sem("r_spread")
        o_normed = sem("o_normed")
        y_in_psum = sem("y_in_psum")
        tsum_ready = sem("tsum_ready")
        x2hat_ready = sem("x2hat_ready")
        x2T_in_psum = sem("x2T_in_psum")
        x2T_ready = sem("x2T_ready")
        f_in_psum = sem("f_in_psum")
        osum_ready = sem("osum_ready")
        bias4_ready = sem("bias4_ready")
        out_ready = sem("out_ready")
        out_stored = [sem("out_stored0"), sem("out_stored1")]

        def over_batches(eng, step, end=B - 2):
            step(0, 0, True, False)
            step(1, 1, True, True)
            with eng.Fori(2, end, 2) as b:
                step(b, 0, True, True)
                step(b + 1, 1, True, True)
            for b in range(end, B):
                step(b, b % 2, b + 1 < B, True)

        def worked_out(eng, count):
            return count if isinstance(count, int) else eng.snap(eng.to_reg(count))

        def p1_at(g, t):
            tiles = [t] if t < ST - 1 else [t, P1 - 1]
            return [((g + 2) // KVH, (g + 2) % KVH, tile) for tile in tiles]

        PV0_AT = 7
        Y_AT = [(1, 8), (1, 9)]
        X2T_AT = [(2, 7), (2, 9)]
        FFN_AT = [(3, 0), (3, 2)]
        MT_AT = 4
        mT_psum = ps_pv[:, 0:P // 2].bitcast(BF16)

        block = ctx.enter_context(nc.Block())

        @block.sync
        def _(sp):
            sp.dma_start(x_ln[:], x_v[0]).then_inc(x_ln_loaded, 16)
            sp.dma_start(wq_sb[:], wq.rearrange("(c p) i -> p c i", p=P)).then_inc(w_loaded, 16)
            sp.dma_start(wkv_sb[0:64, :], wk).then_inc(w_loaded, 16)
            sp.dma_start(wkv_sb[64:128, :], wv).then_inc(w_loaded, 16)
            sp.dma_start(wo_sb[:], wo.rearrange("(c p) i -> p c i", p=P)).then_inc(w_loaded, 16)
            sp.dma_start(wf_sb[:], wf.rearrange("(c p) i -> p c i", p=P)).then_inc(w_loaded, 16)
            sp.dma_start(dish2[0:R, :], disha).then_inc(w_loaded, 16)
            sp.dma_start(dish2[R:2 * R, :], disha).then_inc(w_loaded, 16)

            def stack_k(d, par):
                sp.wait_ge(lo_ready, 3 * d + 1)
                for n, part in enumerate(K_PART):
                    sp.dma_start(KS[DH * n:DH * (n + 1), par, :, :],
                                 k_split[:, part, :]).then_inc(k_stacked, 16)

            def stack_q(d, par):
                sp.wait_ge(lo_ready, 3 * d + 3)
                for n, part in enumerate(Q_PART):
                    sp.dma_start(QS[DH * n:DH * (n + 1), par, :, :].rearrange("p (s m) t -> p s (m t)", m=2),
                                 q_split[:, part, :, :].rearrange("p m t -> p (m t)")).then_inc(q_stacked, 16)

            def stack_m(n, g, par):
                sp.wait_ge(mT_ready, n + 1)
                sp.dma_start(QS[KR:KM, par, HG * g:HG * (g + 1), :].rearrange("p h (t q) -> p (h t) q", q=P),
                             mT_sb[:, g % 2, :]).then_inc(m_stacked, 16)

            def gather_o(d, par):
                sp.wait_ge(oT_evacuated, 4 * d + 4)
                sp.dma_start(zc[:], OT[DH:P:2 * DH, par, :, :].rearrange("p g t -> p (g t)")).then_inc(z_gathered, 16)
                for c in range(HG):
                    sp.dma_start(oraw[64 * (c % 2):64 * (c % 2) + 64, c // 2, :],
                                 OT[32 * c:32 * c + DH, par, :, :]).then_inc(o_gathered, 16)

            def row_r(d):
                sp.wait_ge(recip_done, d + 1)
                sp.dma_start(r_dram.rearrange("c (k e) -> (c k) e", e=64), rc[:]).then_inc(r_rowed, 16)

            def spread_r(d):
                sp.wait_ge(r_rowed, 16 * (d + 1))
                for c in range(HG):
                    sp.dma_start(rrep[64 * (c % 2):64 * (c % 2) + 64, c // 2, :],
                                 r_dram[c].unsqueeze(0).broadcast_to([DH, KVH * S])).then_inc(r_spread, 16)

            def store_out(d, h):
                sp.wait_ge(out_ready, 2 * d + h + 1)
                sp.dma_start(out_v[d][:, 2 * h:2 * h + 2, :], outb[:, 2 * h:2 * h + 2, :]).then_inc(out_stored[h], 16)

            def load_x_res(d):
                if not (isinstance(d, int) and d == 0):
                    sp.wait_ge(tsum_ready, 2 * d)
                sp.dma_start(x_res[:], x_v[d]).then_inc(x_res_loaded, 16)

            def load_x_ln(d):
                sp.wait_ge(xhat_ready, d)
                sp.dma_start(x_ln[:], x_v[d]).then_inc(x_ln_loaded, 16)

            load_x_ln(1)
            stack_k(0, 0)
            stack_q(0, 0)
            stack_m(0, 0, 0)

            def step(b, par, nxt, prev):
                if prev:
                    load_x_res(b - 1)
                if not isinstance(b, int) or b + 2 < B:
                    load_x_ln(b + 2)
                if prev:
                    gather_o(b - 1, 1 - par)
                stack_m(4 * b + 1, 1, par)
                if prev:
                    row_r(b - 1)
                if nxt:
                    stack_k(b + 1, 1 - par)
                if prev:
                    spread_r(b - 1)
                if nxt:
                    stack_q(b + 1, 1 - par)
                stack_m(4 * b + 2, 2, par)
                stack_m(4 * b + 3, 3, par)
                if nxt:
                    stack_m(4 * b + 4, 0, 1 - par)
                if prev:
                    store_out(b - 1, 0)
                    store_out(b - 1, 1)

            over_batches(sp, step, B - 4)
            load_x_res(B - 1)
            gather_o(B - 1, (B - 1) % 2)
            row_r(B - 1)
            spread_r(B - 1)
            store_out(B - 1, 0)
            store_out(B - 1, 1)
            sp.wait_ge(out_stored[0], 16 * B)
            sp.wait_ge(out_stored[1], 16 * B)

        @block.tensor
        def _(pe):
            def transpose_weights():
                pe.wait_ge(const_ready, 7)
                pe.wait_ge(w_loaded, 16 * 7)
                for c in range(NC):
                    for o in range(2):
                        nc.tensor.transpose(ps_p1[0][:, D * c + P * o:D * c + P * (o + 1)],
                                            wq_sb[:, o, P * c:P * (c + 1)], identf[:])
                for c in range(NC):
                    nc.tensor.transpose(ps_p1[1][:, P * c:P * (c + 1)],
                                        wkv_sb[:, P * c:P * (c + 1)], identf[:]).then_inc(w_transposed, 1)
                pe.wait_ge(wo_permuted, 1)
                for c in range(NC):
                    for o in range(2):
                        nc.tensor.transpose(ps_p1[2][:, D * c + P * o:D * c + P * (o + 1)],
                                            wo_perm[:, o, P * c:P * (c + 1)], identf[:])
                for c in range(NC):
                    for o in range(2):
                        last = nc.tensor.transpose(ps_w[1][:, D * c + P * o:D * c + P * (o + 1)],
                                                   wf_sb[:, o, P * c:P * (c + 1)], identf[:])
                last.then_inc(w_transposed, 1)

            def transpose_x(d, c):
                pe.wait_ge(xhat_ready, d + 1)
                for t in range(NT):
                    last = nc.tensor.transpose(ps_w[c][:, P * t:P * (t + 1)], xhat[:, t, P * c:P * (c + 1)], identf[:])
                last.then_inc(xT_in_psum, 1)

            def project(bank, weights):
                for c in range(NC):
                    last = nc.tensor.matmul(ps_w[bank][:], weights(c), xT[:, c, :], start=(c == 0), stop=(c == NC - 1))
                last.then_inc(qkv_in_psum, 1)

            def project_kv(d):
                pe.wait_ge(xT_ready, 2 * d + 2)
                project(0, lambda c: wkvT[:, c, :])

            def project_q0(d):
                project(1, lambda c: wqT[:, c, 0:P])

            def project_q1(d):
                pe.wait_ge(hi_ready, 3 * d + 1)
                project(0, lambda c: wqT[:, c, P:2 * P])

            def transpose_v(d):
                pe.wait_ge(kvT_ready, d + 1)
                pe.wait_ge(resid_ready, 3 * d + 2)
                for t in range(NT):
                    last = nc.tensor.transpose(ps_w[1][:, P * t:P * (t + 1)], kvT_sb[:, P * t:P * (t + 1)], identf[:])
                last.then_inc(v_in_psum, 1)

            def p1_tile(d, g, tile, par):
                at = P1 * g + tile
                per = P1 * KVH
                if tile == 0:
                    if g == 0:
                        pe.wait_ge(k_stacked, 16 * len(K_PART) * (d + 1))
                        pe.wait_ge(q_stacked, 16 * len(Q_PART) * (d + 1))
                if at >= P1S:
                    pe.wait_ge(p1_reduced, per * d + at - P1S + 1)
                elif not (isinstance(d, int) and d == 0):
                    before = max(i for i in range(per) if i % P1S == at)
                    pe.wait_ge(p1_reduced, per * d + before + 1 - per)
                ps = ps_p1[at % P1S]
                if tile < 8:
                    qt, h = 3 - tile // HG, tile % HG
                    heads, n = [h], P * (qt + 1)
                elif tile < 10:
                    qt, heads, n = 1, [2 * (tile - 8), 2 * (tile - 8) + 1], 2 * P
                else:
                    qt, heads, n = 0, list(range(HG)), P
                for i, h in enumerate(heads):
                    nc.tensor.matmul(ps[:, n * i:n * (i + 1)], QS[0:KR, par, HG * g + h, P * qt:P * (qt + 1)],
                                     KS[0:KR, par, g, 0:n], start=(i == 0), stop=False, skip_group_check=True)
                k = len(heads)
                diag = ps[:, 0:n * k].rearrange("p (h k) -> p h k", h=k)[:, :, n - P:n]
                nc.tensor.matmul(diag, identb[:], causal[:].unsqueeze(1).broadcast_to([P, k, P]), start=False,
                                 stop=True, skip_group_check=True).then_inc(p1_in_psum, 1)

            def transpose_m(n):
                pe.wait_ge(m_split, n + 1)
                if not (isinstance(n, int) and n < 2):
                    pe.wait_ge(oT_evacuated, n - 1)
                nc.tensor.transpose(mT_psum, msplit[:].rearrange("p a b -> p (a b)"), identb[:]).then_inc(mT_in_psum, 1)

            def st_tile(b, g, t, par):
                at = ST * g + t
                if t == 0:
                    pe.wait_ge(m_stacked, 16 * (4 * b + g + 1))
                if not (isinstance(b, int) and b == 0 and at < 2):
                    pe.wait_ge(exp_done, ST * KVH * b + at - 1)
                ps = ps_st[t % 2]
                if t < HG:
                    last = nc.tensor.matmul(ps[:], KS[0:KM, par, g, 0:P], QS[0:KM, par, HG * g + t, :],
                                            start=True, stop=True)
                elif t < 2 * HG:
                    h = HG * g + t - HG
                    nc.tensor.matmul(ps[:, P:S], KS[0:KM, par, g, P:2 * P], QS[0:KM, par, h, P:S],
                                     start=True, stop=True)
                    last = nc.tensor.matmul(ps[:, 0:P], KS[0:KM, par, g, 3 * P:S], QS[0:KM, par, h, 3 * P:S],
                                            start=True, stop=True)
                else:
                    h = HG * g + 2 * (t - 2 * HG)
                    last = nc.tensor.matmul(ps[:].rearrange("p (h q) -> p h q", h=2), KS[0:KM, par, g, 2 * P:3 * P],
                                            QS[0:KM, par, h:h + 2, 2 * P:S], start=True, stop=True)
                last.then_inc(st_in_psum, 1)

            def pv(n, g, par, kt, v_count=None, bank_held=False):
                tile = {0: 0, 1: HG, 3: HG, 2: 2 * HG}[kt]
                pe.wait_ge(masked, 3 * n + {0: 1, 1: 2, 3: 2, 2: 3}[kt])
                if kt == 0:
                    if g == 0:
                        pe.wait_ge(v_ready, v_count)
                    if bank_held:
                        pe.wait_ge(mT_ready, n + 2)
                    else:
                        pe.wait_ge(oT_evacuated, n)
                for h in range(HG):
                    slot = ST * (g % 2) + tile + (h // 2 if kt == 2 else h)
                    lo = {0: 0, 1: P, 3: 0, 2: 2 * P * (h % 2)}[kt]
                    width = S - P * kt
                    last = nc.tensor.matmul(ps_pv[32 * h:32 * (h + 1), P * kt:S], V1[:, par, kt, g, :],
                                            PT[:, slot, lo:lo + width], start=(kt == 0), stop=(kt == 2),
                                            tile_position=(0, 32 * h), skip_group_check=True)
                if kt == 2:
                    last.then_inc(pv_done, 1)

            def out_project(d, h):
                if h == 0:
                    pe.wait_ge(o_normed, 2 * d + 2)
                for t in range(2):
                    for c in range(NC):
                        last = nc.tensor.matmul(ps_w[h][:, D * t:D * (t + 1)],
                                                oT[:, c, P * (2 * h + t):P * (2 * h + t + 1)], woT[:, c, :],
                                                start=(c == 0), stop=(c == NC - 1), skip_group_check=True)
                last.then_inc(y_in_psum, 1)

            def transpose_x2(d, h):
                pe.wait_ge(x2hat_ready, 2 * d + h + 1)
                for c in range(NC):
                    for t in range(2):
                        last = nc.tensor.transpose(ps_w[h][:, D * c + P * t:D * c + P * (t + 1)],
                                                   x2hat[:, 2 * h + t, P * c:P * (c + 1)], identf[:])
                last.then_inc(x2T_in_psum, 1)

            def ffn(d, h):
                pe.wait_ge(x2T_ready, 2 * d + h + 1)
                for t in range(2):
                    for c in range(NC):
                        last = nc.tensor.matmul(ps_w[h][:, D * t:D * (t + 1)],
                                                x2T[:, c, P * (2 * h + t):P * (2 * h + t + 1)], wfT[:, c, :],
                                                start=(c == 0), stop=(c == NC - 1), skip_group_check=True)
                last.then_inc(f_in_psum, 1)

            transpose_weights()
            pe.wait_ge(w_ready, 4)
            for c in range(NC):
                transpose_x(0, c)
            project_kv(0)
            project_q0(0)
            project_q1(0)
            transpose_v(0)
            for tile in range(P1):
                p1_tile(0, 0, tile, 0)
            for tile in range(P1):
                p1_tile(0, 1, tile, 0)
                if tile == MT_AT:
                    transpose_m(0)

            def step(b, par, nxt, prev):
                n0 = 4 * b
                first = isinstance(b, int) and b == 0
                for g in range(KVH):
                    n = n0 + g
                    for t in range(ST):
                        st_tile(b, g, t, par)
                        for ahead, pg, tile in p1_at(g, t):
                            if ahead == 0 or nxt:
                                p1_tile(b + ahead, pg, tile, par if ahead == 0 else 1 - par)
                        if not (first and g == 0):
                            if t == 1:
                                pv(n - 1, (g - 1) % KVH, par if g else 1 - par, 1)
                                pv(n - 1, (g - 1) % KVH, par if g else 1 - par, 3)
                            if t == 2:
                                pv(n - 1, (g - 1) % KVH, par if g else 1 - par, 2)
                        if t == MT_AT and (g < 3 or nxt):
                            transpose_m(n + 1)
                        if t == PV0_AT:
                            pv(n, g, par, 0, b + 1, g < 3 or nxt)
                        if nxt:
                            if (g, t) == (0, 0):
                                if prev:
                                    pe.wait_ge(osum_ready, 2 * b - 1)
                                transpose_x(b + 1, 0)
                            if (g, t) == (0, 1):
                                if prev:
                                    pe.wait_ge(osum_ready, 2 * b)
                                else:
                                    pe.wait_ge(v_ready, 1)
                                transpose_x(b + 1, 1)
                            if (g, t) == (0, 3):
                                project_kv(b + 1)
                            if (g, t) == (0, 4):
                                project_q0(b + 1)
                            if (g, t) == (0, 6):
                                project_q1(b + 1)
                            if (g, t) == (0, 8):
                                transpose_v(b + 1)
                        if prev:
                            if (g, t) == Y_AT[0]:
                                if nxt:
                                    pe.wait_ge(resid_ready, 3 * (b + 1) + 3)
                                else:
                                    pe.wait_ge(osum_ready, 2 * b - 1)
                                out_project(b - 1, 0)
                            if (g, t) == Y_AT[1]:
                                if nxt:
                                    pe.wait_ge(v_ready, b + 2)
                                else:
                                    pe.wait_ge(osum_ready, 2 * b)
                                out_project(b - 1, 1)
                            for h in range(2):
                                if (g, t) == X2T_AT[h]:
                                    transpose_x2(b - 1, h)
                                if (g, t) == FFN_AT[h]:
                                    ffn(b - 1, h)

            over_batches(pe, step)
            last_g, last_par = KVH - 1, (B - 1) % 2
            for kt in (1, 3, 2):
                pv(KVH * B - 1, last_g, last_par, kt)
            pe.wait_ge(osum_ready, 2 * (B - 1) + 2)
            out_project(B - 1, 0)
            out_project(B - 1, 1)
            for h in range(2):
                transpose_x2(B - 1, h)
            for h in range(2):
                ffn(B - 1, h)

        @block.scalar
        def _(act):
            def copy_xT(d, c):
                act.wait_ge(xT_in_psum, 2 * d + c + 1)
                nc.scalar.copy(xT[:, c, :], ps_w[c][:]).then_inc(xT_ready, 1)

            def split_hi_k(d):
                act.wait_ge(qkv_in_psum, 3 * d + 1)
                if not (isinstance(d, int) and d == 0):
                    act.wait_ge(k_stacked, 16 * len(K_PART) * d)
                nc.scalar.copy(kvT_sb[:], ps_w[0][:]).then_inc(kvT_ready, 1)
                nc.scalar.copy(k_split[:, HI, :], ps_w[0][0:64, :]).then_inc(hi_ready, 1)

            def split_hi_q(d, half):
                act.wait_ge(qkv_in_psum, 3 * d + 2 + half)
                if not (isinstance(d, int) and d == 0):
                    act.wait_ge(q_stacked, 16 * len(Q_PART) * d)
                nc.scalar.mul(q_split[:, HI, half, :], ps_w[1 - half][:], SCALE).then_inc(hi_ready, 1)

            def copy_v(d, par):
                act.wait_ge(v_in_psum, d + 1)
                nc.scalar.copy(V1[:, par, :, :, 0:DH],
                               ps_w[1][:].rearrange("p (t k g d) -> p t k g d", t=NT, k=2, d=DH)[:, :, 1]
                               ).then_inc(v_ready, 1)

            def copy_mT(n, g):
                act.wait_ge(mT_in_psum, n + 1)
                if not (isinstance(n, int) and n < 2):
                    act.wait_ge(m_stacked, 16 * (n - 1))
                nc.scalar.copy(mT_sb[:, g % 2, :], mT_psum[0:3 * H, :]).then_inc(mT_ready, 1)

            def exp_tile(b, g, t):
                act.wait_ge(st_in_psum, ST * (KVH * b + g) + t + 1)
                if t == 0 and not (isinstance(b, int) and b == 0 and g < 2):
                    act.wait_ge(pv_done, 4 * b + g - 1)
                nc.scalar.activation(PT[:, ST * (g % 2) + t, :], ps_st[t % 2][:], ACT.Exp).then_inc(exp_done, 1)

            def copy_oT(n, g, par, d):
                act.wait_ge(pv_done, n + 1)
                if g == 0 and not (isinstance(d, int) and d < 2):
                    act.wait_ge(z_gathered, 16 * (d - 1))
                    act.wait_ge(o_gathered, 64 * (d - 1))
                nc.scalar.copy(OT[:, par, g, :], ps_pv[:]).then_inc(oT_evacuated, 1)

            def apply_ln3(d, h):
                act.wait_ge(ln3.shift_done, 2 * d + h + 1)
                for t in (2 * h, 2 * h + 1):
                    last = nc.scalar.activation(x2hat[:, t, :], tsum[:, t, :], ACT.Identity,
                                                bias=ln3.shift[:, t:t + 1], scale=ln3.rstd[:, t:t + 1])
                last.then_inc(x2hat_ready, 1)

            def copy_x2T(d, h):
                act.wait_ge(x2T_in_psum, 2 * d + h + 1)
                nc.scalar.copy(x2T[:, :, 2 * P * h:2 * P * (h + 1)],
                               ps_w[h][:].rearrange("p (c q) -> p c q", c=NC)).then_inc(x2T_ready, 1)

            def finish_out(d, h):
                act.wait_ge(bias4_ready, 2 * d + h + 1)
                if not (isinstance(d, int) and d == 0):
                    act.wait_ge(out_stored[h], 16 * d)
                for t in (2 * h, 2 * h + 1):
                    last = nc.scalar.activation(outb[:, t, :], osum[:, t, :], ACT.Identity, bias=bias4[:, t:t + 1])
                last.then_inc(out_ready, 1)

            act.wait_ge(w_ready, 4)
            copy_xT(0, 0)
            copy_xT(0, 1)
            split_hi_k(0)
            split_hi_q(0, 0)
            split_hi_q(0, 1)
            copy_v(0, 0)
            copy_mT(0, 0)

            def step(b, par, nxt, prev):
                n0 = 4 * b
                first = isinstance(b, int) and b == 0
                for g in range(KVH):
                    for t in range(ST):
                        exp_tile(b, g, t)
                        if t == 3 and not (first and g == 0):
                            copy_oT(n0 + g - 1, (g - 1) % KVH, par if g else 1 - par, b if g else b - 1)
                        if t == MT_AT + 1 and (g < 3 or nxt):
                            copy_mT(n0 + g + 1, (g + 1) % KVH)
                        if nxt:
                            if (g, t) == (0, 1):
                                copy_xT(b + 1, 0)
                            if (g, t) == (0, 2):
                                copy_xT(b + 1, 1)
                            if (g, t) == (0, 4):
                                split_hi_k(b + 1)
                            if (g, t) == (0, 5):
                                split_hi_q(b + 1, 0)
                            if (g, t) == (0, 7):
                                split_hi_q(b + 1, 1)
                            if (g, t) == (0, 9):
                                copy_v(b + 1, 1 - par)
                        if prev:
                            if (g, t) == (2, 5):
                                apply_ln3(b - 1, 0)
                            if (g, t) == (2, 7):
                                apply_ln3(b - 1, 1)
                            if (g, t) == (2, 8):
                                copy_x2T(b - 1, 0)
                            if (g, t) == (3, 0):
                                copy_x2T(b - 1, 1)
                            if (g, t) == (3, 7):
                                finish_out(b - 1, 0)
                            if (g, t) == (3, 9):
                                finish_out(b - 1, 1)

            over_batches(act, step)
            copy_oT(KVH * B - 1, KVH - 1, (B - 1) % 2, B - 1)
            apply_ln3(B - 1, 0)
            apply_ln3(B - 1, 1)
            copy_x2T(B - 1, 0)
            copy_x2T(B - 1, 1)
            finish_out(B - 1, 0)
            finish_out(B - 1, 1)

        @block.vector
        def _(dve):
            def constants():
                nc.vector.memset(msplit[:], 0.0).then_inc(const_ready, 1)
                nc.vector.memset(powexp[:], -0.5).then_inc(const_ready, 1)
                nc.vector.memset(KS[KR:KM], 1.0).then_inc(const_ready, 1)
                nc.vector.memset(V1[:, :, :, :, DH:2 * DH], 1.0).then_inc(const_ready, 1)

            def permute_wo():
                dve.wait_ge(w_loaded, 16 * 7)
                for o in range(2):
                    for cc in range(NC):
                        src = wo_sb[:, o, :].rearrange("p (g c d) -> p c d g", g=KVH, c=HG)[:, 2 * cc:2 * cc + 2, :, :]
                        dst = wo_perm[:, o, P * cc:P * (cc + 1)].rearrange("p (c d g) -> p c d g", c=2, d=DH)
                        last = nc.vector.tensor_copy(dst, src)
                last.then_inc(wo_permuted, 1)

            def lay_out_weights():
                dve.wait_ge(w_transposed, 2)
                for c in range(NC):
                    nc.vector.tensor_copy(
                        wqT[:, c, :].rearrange("p (m d s) -> p m d s", m=2, d=DH),
                        ps_p1[0][:, D * c:D * (c + 1)].rearrange("p (s m d) -> p m d s", s=8, m=2))
                dve.wait_ge(w_transposed, 2)
                for c in range(NC):
                    nc.vector.tensor_copy(wkvT[:, c, 0:64].rearrange("p (d g) -> p d g", d=DH),
                                          ps_p1[1][:, P * c:P * c + 64].rearrange("p (g d) -> p d g", g=KVH))
                    last = nc.vector.tensor_copy(wkvT[:, c, 64:P], ps_p1[1][:, P * c + 64:P * (c + 1)])
                last.then_inc(w_ready, 2)
                dve.wait_ge(w_transposed, 3)
                nc.vector.tensor_copy(woT[:].rearrange("p c o -> p (c o)"), ps_p1[2][:]).then_inc(w_ready, 1)
                nc.vector.tensor_tensor(wfT[:], ps_w[1][:].rearrange("p (c o) -> p c o", c=NC),
                                        dish2[:].unsqueeze(1).broadcast_to([P, NC, D]), ALU.add).then_inc(w_ready, 1)

            def stats(ln, src, tiles, done):
                for t in tiles:
                    last = nc.vector.bn_stats(ln.stats[:, t, :], src(t))
                last.then_inc(ln.stats_done, 1)

            def aggregate(ln, tiles, done):
                done_by = worked_out(dve, done + 1)
                dve.wait_ge(w_loaded, 16 * 7)
                dve.wait_ge(ln.stats_done, done_by)
                for t in tiles:
                    last = nc.vector.bn_aggr(ln.mv[:, t, :], ln.stats[:, t, :])
                last.then_inc(ln.var_done, 1)

            def shift(ln, h, done):
                a, b = 2 * h, 2 * h + 2
                dve.wait_ge(ln.rstd_done, done + 1)
                nc.vector.scalar_tensor_tensor(ln.shift[:, a:b], ln.mv[:, a:b, 0], -1.0, ln.rstd[:, a:b],
                                               ALU.mult, ALU.mult).then_inc(ln.shift_done, 1)

            def ln1_stats(d):
                dve.wait_ge(x_ln_loaded, 16 * (d + 1))
                stats(ln1, lambda t: x_ln[:, t, :], range(NT), d)
                aggregate(ln1, range(NT), d)

            def ln1_apply(d):
                dve.wait_ge(ln1.rstd_done, d + 1)
                if not (isinstance(d, int) and d == 0):
                    dve.wait_ge(xT_in_psum, 2 * d)
                for t in range(NT):
                    last = nc.vector.tensor_scalar(xhat[:, t, :], x_ln[:, t, :], ln1.mv[:, t, 0:1],
                                                   ln1.rstd[:, t:t + 1], ALU.subtract, ALU.mult)
                last.then_inc(xhat_ready, 1)

            def split_rest(d, i):
                dve.wait_ge(hi_ready, 3 * d + i + 1)
                if i == 0:
                    rows, ps, scale, part = 64, kvT_sb, 1.0, lambda p: k_split[:, p, :]
                    dve.wait_ge(kvT_ready, d + 1)
                else:
                    rows, ps, scale = P, ps_w[2 - i], SCALE
                    part = lambda p: q_split[:, p, i - 1, :]
                if not (isinstance(d, int) and d == 0):
                    dve.wait_ge(lo_ready, 3 * d + i - 2)
                nc.vector.scalar_tensor_tensor(resid[0:rows, i, :], ps[0:rows, :], scale, part(HI),
                                               ALU.mult, ALU.subtract).then_inc(resid_ready, 1)
                dve.wait_ge(resid_ready, 3 * d + i + 1)
                nc.vector.tensor_copy(part(MID), resid[0:rows, i, :]).then_inc(mid_ready, 1)

            def p1_reduce(d, g, tile):
                at = P1 * g + tile
                n = 4 * d + g
                if tile == 0 and not (isinstance(d, int) and d == 0 and g < 2):
                    dve.wait_ge(m_split, n - 1)
                dve.wait_ge(p1_in_psum, P1 * n + tile + 1)
                ps = ps_p1[at % P1S]
                if tile < 8:
                    qt, h0, k = 3 - tile // HG, tile % HG, 1
                elif tile < 10:
                    qt, h0, k = 1, 2 * (tile - 8), 2
                else:
                    qt, h0, k = 0, 0, HG
                w = P * (qt + 1)
                m = mneg[:, g % 2, :].rearrange("p (h t) -> p h t", h=HG)[:, h0:h0 + k, qt]
                nc.vector.tensor_reduce(m, ps[:, 0:w * k].rearrange("p (h k) -> p h k", h=k), AX.X, ALU.max,
                                        negate=True).then_inc(p1_reduced, 1)

            def recip(d):
                dve.wait_ge(z_gathered, 16 * (d + 1))
                if not (isinstance(d, int) and d == 0):
                    dve.wait_ge(r_rowed, 16 * d)
                nc.vector.reciprocal(rc[:], zc[:]).then_inc(recip_done, 1)

            def ln2_stats(d, h):
                dve.wait_ge(y_in_psum, 2 * d + h + 1)
                stats(ln2, lambda t: ps_w[h][:, D * (t % 2):D * (t % 2 + 1)], (2 * h, 2 * h + 1), 2 * d + h)
                aggregate(ln2, (2 * h, 2 * h + 1), 2 * d + h)

            def ln2_apply(d, h):
                if h == 0:
                    dve.wait_ge(x_res_loaded, 16 * (d + 1))
                    if not (isinstance(d, int) and d == 0):
                        dve.wait_ge(x2hat_ready, 2 * d)
                dve.wait_ge(ln2.rstd_done, 2 * d + h + 1)
                for t in (2 * h, 2 * h + 1):
                    last = nc.vector.scalar_tensor_tensor(tsum[:, t, :], ps_w[h][:, D * (t % 2):D * (t % 2 + 1)],
                                                          ln2.rstd[:, t:t + 1], x_res[:, t, :], ALU.mult, ALU.add)
                last.then_inc(tsum_ready, 1)
                shift(ln2, h, 2 * d + h)

            def ln3_stats(d, h):
                dve.wait_ge(tsum_ready, 2 * d + h + 1)
                stats(ln3, lambda t: tsum[:, t, :], (2 * h, 2 * h + 1), 2 * d + h)
                aggregate(ln3, (2 * h, 2 * h + 1), 2 * d + h)

            def ln4_stats(d, h):
                dve.wait_ge(f_in_psum, 2 * d + h + 1)
                stats(ln4, lambda t: ps_w[h][:, D * (t % 2):D * (t % 2 + 1)], (2 * h, 2 * h + 1), 2 * d + h)
                aggregate(ln4, (2 * h, 2 * h + 1), 2 * d + h)

            def ln4_apply(d, h):
                a, b = 2 * h, 2 * h + 2
                dve.wait_ge(ln4.rstd_done, 2 * d + h + 1)
                if not (isinstance(d, int) and d == 0):
                    dve.wait_ge(out_ready, 2 * d)
                for t in range(a, b):
                    last = nc.vector.scalar_tensor_tensor(osum[:, t, :], ps_w[h][:, D * (t % 2):D * (t % 2 + 1)],
                                                          ln4.rstd[:, t:t + 1], tsum[:, t, :], ALU.mult, ALU.add)
                last.then_inc(osum_ready, 1)
                shift(ln4, h, 2 * d + h)
                dve.wait_ge(ln4.shift_done, 2 * d + h + 1)
                dve.wait_ge(osum_ready, 2 * d + h + 3)
                nc.vector.tensor_tensor(bias4[:, a:b], ln4.shift[:, a:b], ln2.shift[:, a:b],
                                        ALU.add).then_inc(bias4_ready, 1)

            dve.sem_inc(osum_ready, 2)
            constants()
            permute_wo()
            ln1_stats(0)
            ln1_apply(0)
            lay_out_weights()
            for i in range(3):
                split_rest(0, i)
            ln1_stats(1)
            for tile in range(P1):
                p1_reduce(0, 0, tile)
            for tile in range(P1):
                p1_reduce(0, 1, tile)
            ln1_apply(1)

            def step(b, par, nxt, prev):
                for g in range(KVH):
                    for t in range(ST):
                        for ahead, pg, tile in p1_at(g, t):
                            if ahead == 0 or nxt:
                                p1_reduce(b + ahead, pg, tile)
                        if nxt:
                            if (g, t) == (0, 5):
                                split_rest(b + 1, 0)
                            if (g, t) == (0, 6):
                                split_rest(b + 1, 1)
                            if (g, t) == (0, 8):
                                split_rest(b + 1, 2)
                            if not isinstance(b, int) or b + 2 < B:
                                if (g, t) == (3, 1):
                                    ln1_stats(b + 2)
                                if (g, t) == (3, 7):
                                    ln1_apply(b + 2)
                        if prev:
                            if (g, t) == (0, 7):
                                recip(b - 1)
                            if (g, t) == (1, 9):
                                ln2_stats(b - 1, 0)
                            if (g, t) == (2, 0):
                                ln2_stats(b - 1, 1)
                            if (g, t) == (2, 1):
                                ln2_apply(b - 1, 0)
                                ln3_stats(b - 1, 0)
                            if (g, t) == (2, 3):
                                ln2_apply(b - 1, 1)
                                ln3_stats(b - 1, 1)
                            if (g, t) == (2, 4):
                                shift(ln3, 0, 2 * (b - 1))
                            if (g, t) == (2, 6):
                                shift(ln3, 1, 2 * (b - 1) + 1)
                            if (g, t) == (3, 2):
                                ln4_stats(b - 1, 0)
                            if (g, t) == (3, 4):
                                ln4_stats(b - 1, 1)
                            if (g, t) == (3, 5):
                                ln4_apply(b - 1, 0)
                            if (g, t) == (3, 8):
                                ln4_apply(b - 1, 1)

            over_batches(dve, step)
            recip(B - 1)
            for h in range(2):
                ln2_stats(B - 1, h)
            for h in range(2):
                ln2_apply(B - 1, h)
                ln3_stats(B - 1, h)
            for h in range(2):
                shift(ln3, h, 2 * (B - 1) + h)
            for h in range(2):
                ln4_stats(B - 1, h)
            for h in range(2):
                ln4_apply(B - 1, h)

        @block.gpsimd
        def _(pool):
            def constants():
                nc.gpsimd.memset(identf[:], 0.0).then_inc(const_zeroed, 1)
                nc.gpsimd.memset(identb[:], 0.0).then_inc(const_zeroed, 1)
                nc.gpsimd.memset(causal[:], 0.0).then_inc(const_zeroed, 1)
                pool.wait_ge(const_zeroed, 3)
                for m in (identf, identb):
                    nc.gpsimd.affine_select(out=m[:], in_=m[:], compare_op=ALU.not_equal, fill=1.0, base=0,
                                            pattern=[[-1, P]], channel_multiplier=1).then_inc(const_ready, 1)
                nc.gpsimd.affine_select(out=causal[:], in_=causal[:], compare_op=ALU.is_ge, fill=NEG, base=0,
                                        pattern=[[-1, P]], channel_multiplier=1).then_inc(const_ready, 1)

            def rstd(ln, tiles, done):
                a, b = tiles
                done_by = worked_out(pool, done + 1)
                pool.wait_ge(const_ready, 7)
                pool.wait_ge(ln.var_done, done_by)
                nc.gpsimd.tensor_scalar(ln.veps[:, a:b], ln.mv[:, a:b, 1], EPS, None,
                                        ALU.add).then_inc(ln.eps_done, 1)
                pool.wait_ge(ln.eps_done, done + 1)
                nc.gpsimd.tensor_tensor(ln.rstd[:, a:b], ln.veps[:, a:b], powexp[:, a:b],
                                        ALU.pow).then_inc(ln.rstd_done, 1)

            def split_lo(d, i):
                pool.wait_ge(mid_ready, 3 * d + i + 1)
                rows = 64 if i == 0 else P
                part = (lambda p: k_split[:, p, :]) if i == 0 else (lambda p: q_split[:, p, i - 1, :])
                nc.gpsimd.tensor_tensor(part(LO), resid[0:rows, i, :], part(MID), ALU.subtract).then_inc(lo_ready, 1)

            def split_max(n, g):
                maxima_by, parts_by = worked_out(pool, P1 * (n + 1)), worked_out(pool, n)
                pool.wait_ge(const_ready, 7)
                pool.wait_ge(p1_reduced, maxima_by)
                if not (isinstance(n, int) and n == 0):
                    pool.wait_ge(mT_in_psum, parts_by)
                m = mneg[:, g % 2, :]
                nc.gpsimd.tensor_copy(msplit[:, HI, :], m).then_inc(m_hi, 1)
                pool.wait_ge(m_hi, n + 1)
                nc.gpsimd.tensor_tensor(mres[:], m, msplit[:, HI, :], ALU.subtract).then_inc(m_res, 1)
                done_by = worked_out(pool, n + 1)
                pool.wait_ge(const_ready, 7)
                pool.wait_ge(m_res, done_by)
                nc.gpsimd.tensor_copy(msplit[:, MID, :], mres[:]).then_inc(m_mid, 1)
                pool.wait_ge(m_mid, n + 1)
                nc.gpsimd.tensor_tensor(msplit[:, LO, :], mres[:], msplit[:, MID, :], ALU.subtract).then_inc(m_split, 1)

            def mask(n, g, kind):
                s0 = ST * (g % 2)
                first, count = [(0, HG), (HG, HG), (2 * HG, 2)][kind]
                done_by = worked_out(pool, ST * n + first + count)
                pool.wait_ge(const_ready, 7)
                pool.wait_ge(exp_done, done_by)
                v = PT[:, s0 + first:s0 + first + count, :]
                if kind == 0:
                    v, blocks = v[:, :, 0:P], HG
                elif kind == 1:
                    v, blocks = v[:, :, 0:2 * P], 2 * HG
                else:
                    v, blocks = v.rearrange("p s (a q) -> p (s a) q", a=2)[:, :, 0:P], HG
                nc.gpsimd.affine_select(out=v, in_=v, compare_op=ALU.is_ge, fill=0.0, base=0,
                                        pattern=[[0, blocks], [1, P]],
                                        channel_multiplier=-1).then_inc(masked, 1)

            def norm_o(d, par):
                pool.wait_ge(r_spread, 64 * (d + 1))
                pool.wait_ge(o_gathered, 64 * (d + 1))
                if not (isinstance(d, int) and d == 0):
                    pool.wait_ge(y_in_psum, 2 * d)
                for c in range(NC):
                    nc.gpsimd.tensor_tensor(oT[:, c, :], oraw[:, c, :], rrep[:, c, :],
                                            ALU.mult).then_inc(o_normed, 1)

            constants()
            rstd(ln1, (0, NT), 0)
            for i in range(3):
                split_lo(0, i)
            rstd(ln1, (0, NT), 1)
            split_max(0, 0)

            def step(b, par, nxt, prev):
                n0 = 4 * b
                for g in range(KVH):
                    n = n0 + g
                    if g == 2 and prev:
                        rstd(ln2, (0, 2), 2 * (b - 1))
                        rstd(ln2, (2, 4), 2 * (b - 1) + 1)
                        rstd(ln3, (0, 2), 2 * (b - 1))
                    if g < 3 or nxt:
                        split_max(n + 1, (g + 1) % KVH)
                    if g == 3 and (not isinstance(b, int) or b + 2 < B):
                        rstd(ln1, (0, NT), b + 2)
                    if g == 3 and prev:
                        rstd(ln4, (0, 2), 2 * (b - 1))
                    mask(n, g, 0)
                    if g == 0 and nxt:
                        split_lo(b + 1, 0)
                        split_lo(b + 1, 1)
                    if g == 2 and prev:
                        rstd(ln3, (2, 4), 2 * (b - 1) + 1)
                    if g == 3 and prev:
                        rstd(ln4, (2, 4), 2 * (b - 1) + 1)
                    if g == 1 and prev:
                        norm_o(b - 1, 1 - par)
                    mask(n, g, 1)
                    if g == 0 and nxt:
                        split_lo(b + 1, 2)
                    mask(n, g, 2)

            over_batches(pool, step)
            norm_o(B - 1, (B - 1) % 2)
            for h in range(2):
                rstd(ln2, (2 * h, 2 * h + 2), 2 * (B - 1) + h)
            for h in range(2):
                rstd(ln3, (2 * h, 2 * h + 2), 2 * (B - 1) + h)
            for h in range(2):
                rstd(ln4, (2 * h, 2 * h + 2), 2 * (B - 1) + h)


_INS = ["L0_attn_x", "L0_attn_Wq", "L0_attn_Wk", "L0_attn_Wv", "L0_attn_Wo", "L0_ffn_weight", "L0_ffn_disha"]


def kernel(**inputs):
    import numpy as np
    import concourse.bacc as bacc
    from concourse.bass_utils import run_bass_kernel_spmd

    nc = bacc.Bacc("TRN2", target_bir_lowering=False, num_devices=1)
    arrays, args = {}, []
    for name in _INS:
        a = np.ascontiguousarray(inputs[name])
        arrays[name] = a
        args.append(nc.dram_tensor(name, a.shape, mybir.dt.from_np(a.dtype), kind="ExternalInput").ap())
    shape = inputs["L0_attn_x"].shape
    out = nc.dram_tensor("block_out", shape, mybir.dt.float32, kind="ExternalOutput").ap()
    sandwich_kernel(nc, *args, out)
    return run_bass_kernel_spmd(nc, [arrays], core_ids=[0]).results[0]["block_out"]
```

```python
import concourse.bass as bass
from concourse import mybir
from contextlib import ExitStack

AT = {
    "pe_pv1": 0, "pe_pv3": 1, "pe_pv2": 2, "pe_mT": 5, "pe_pv0": 8, "pe_xT0": 1, "pe_xT1": 1, "pe_kv0": 4,
    "pe_kv1": 4, "pe_q00": 5, "pe_q01": 6, "pe_q10": 5, "pe_q11": 10, "pe_v": 13, "pe_y0": 19, "pe_y1": 19,
    "pe_y2": 23, "pe_y3": 25, "pe_x2T0": 29, "pe_x2T1": 35, "pe_ffn0": 32, "pe_ffn1": 33, "pe_ffn2": 35,
    "pe_ffn3": 37,
    "act_oT": 3, "act_mT": 6, "act_xT0": 0, "act_xT1": 2, "act_k": 3, "act_q0": 8, "act_q1": 11, "act_v": 17,
    "act_z": 4, "act_row": 8, "act_spread": 10, "act_ln3_0": 27, "act_ln3_1": 32, "act_x2T0": 31, "act_x2T1": 33,
    "act_out0": 37, "act_out1": 39, "act_mid0": 6, "act_mid1": 9, "act_mid2": 13,
    "dve_k": 5, "dve_q0": 8, "dve_q1": 12, "dve_ln1_0": 15, "dve_ln1_1": 16, "dve_xhat0": 19, "dve_xhat1": 20,
    "dve_recip": 6, "dve_ln2_0": 22, "dve_ln2_1": 25, "dve_tsum0": 25, "dve_tsum1": 29, "dve_ln3_0": 25,
    "dve_ln3_1": 29, "dve_sh3_0": 27, "dve_sh3_1": 32, "dve_ln4_0": 34, "dve_ln4_1": 37, "dve_sh4_0": 36,
    "dve_sh4_1": 39, "dve_ag1_0": 16, "dve_ag1_1": 16, "dve_ag2_0": 22, "dve_ag2_1": 26, "dve_ag3_0": 25,
    "dve_ag3_1": 29, "dve_ag4_0": 35, "dve_ag4_1": 38, "dve_bias0": 36, "dve_bias1": 39,
    "pool_m": 1, "pool_k": 6, "pool_q0": 8, "pool_q1": 16, "pool_o0": 12, "pool_o1": 16, "pool_ln2_0": 22,
    "pool_ln2_1": 27, "pool_ln3_0": 26, "pool_ln3_1": 30, "pool_ln4_0": 35, "pool_ln4_1": 38, "pool_ln1": 18,
    "pool_ABC": (4, 8, 9), "pool_out0": 39, "pool_out1": 40,
    "sp_x_res": 1, "sp_x_ln": 2, "sp_oraw": 3, "sp_m": 6, "sp_k": (5, 7, 8), "sp_q": (12, 14, 14), "sp_out0": 38,
    "sp_out1": 40,
}


def sandwich_kernel(nc, x, wq, wk, wv, wo, wf, disha, out):
    F32, BF16 = mybir.dt.float32, mybir.dt.bfloat16
    ALU = mybir.AluOpType
    ACT = mybir.ActivationFunctionType
    AX = mybir.AxisListType

    B, S, D = x.shape
    H, DH, P = 16, 16, 128
    KVH = wk.shape[0] // DH
    HG = H // KVH
    R = disha.shape[0]
    NT = S // P
    NC = D // P
    SCALE = DH ** -0.5
    EPS = 1e-5
    NEG = -3.0e38
    HI, MID, LO = 0, 1, 2
    Q_PART = [HI, HI, MID, HI, MID, LO]
    K_PART = [HI, MID, HI, LO, MID, HI]
    KR = len(Q_PART) * DH
    KM = KR + 3
    ST = 10
    P1 = 11
    P1S = 3

    x_v = x.rearrange("b (t p) f -> b p t f", p=P)
    out_v = out.rearrange("b (t p) f -> b p t f", p=P)

    ctx = ExitStack()
    with ctx:
        def sb(name, shape, dt=F32):
            return ctx.enter_context(nc.sbuf_tensor(name, shape, dt))

        def sem(name):
            return ctx.enter_context(nc.semaphore(name))

        wq_sb = sb("wq_sb", [P, 2, D])
        wkv_sb = sb("wkv_sb", [P, D])
        wo_sb = sb("wo_sb", [P, 2, D])
        wo_perm = sb("wo_perm", [P, 2, D])
        wf_sb = sb("wf_sb", [P, 2, D])
        dish2 = sb("dish2", [P, D])
        wqT = sb("wqT", [P, NC, D])
        wkvT = sb("wkvT", [P, NC, P])
        woT = sb("woT", [P, NC, D])
        wfT = sb("wfT", [P, NC, D])
        identf = sb("identf", [P, P])
        identb = sb("identb", [P, P], BF16)
        causal = sb("causal", [P, P], BF16)
        powexp = sb("powexp", [P, NT])

        x_ln = sb("x_ln", [P, NT, D])
        xhat = sb("xhat", [P, NT, D])
        xT = sb("xT", [P, NC, S])
        q_split = sb("q_split", [P, 3, 2, S], BF16)
        k_split = sb("k_split", [64, 3, S], BF16)
        resid = sb("resid", [P, 3, S])
        kvT_sb = sb("kvT_sb", [P, S])
        QS = sb("QS", [P, 2, H, S], BF16)
        KS = sb("KS", [P, 2, KVH, S], BF16)
        V1 = sb("V1", [P, 2, NT, KVH, 2 * DH])

        mneg = sb("mneg", [P, 2, H])
        mres = sb("mres", [P, H])
        msplit = sb("msplit", [P, P // H, H], BF16)
        mT_sb = sb("mT_sb", [3 * H, 2, P], BF16)
        PT = sb("PT", [P, 2 * ST, S])
        OT = sb("OT", [P, 2, KVH, S])

        zc = sb("zc", [P, 64])
        rc = sb("rc", [P, 64])
        r_dram = nc.dram_tensor("r_scratch", (HG, KVH * S), F32, kind="Internal").ap()
        rrep = sb("rrep", [P, NC, S])
        oraw = sb("oraw", [P, NC, S])
        oT = sb("oT", [P, NC, S])
        x_res = sb("x_res", [P, NT, D])
        tsum = sb("tsum", [P, NT, D])
        x2hat = sb("x2hat", [P, NT, D])
        x2T = sb("x2T", [P, NC, S])
        osum = sb("osum", [P, NT, D])
        outb = sb("outb", [P, NT, D])

        class Norm:
            def __init__(self, n):
                self.stats = sb(f"ln{n}_stats", [P, NT, 6])
                self.mv = sb(f"ln{n}_mv", [P, NT, 2])
                self.veps = sb(f"ln{n}_veps", [P, NT])
                self.rstd = sb(f"ln{n}_rstd", [P, NT])
                self.shift = sb(f"ln{n}_shift", [P, NT])
                self.stats_done = sem(f"ln{n}_stats_done")
                self.var_done = sem(f"ln{n}_var_done")
                self.eps_done = sem(f"ln{n}_eps_done")
                self.rstd_done = sem(f"ln{n}_rstd_done")
                self.shift_done = sem(f"ln{n}_shift_done")

        ln1, ln2, ln3, ln4 = Norm(1), Norm(2), Norm(3), Norm(4)
        bias4 = sb("bias4", [P, NT])

        ps_st = [ctx.enter_context(nc.psum_tensor(f"ps_st{i}", [P, S], F32)) for i in range(2)]
        ps_p1 = [ctx.enter_context(nc.psum_tensor(f"ps_p1{i}", [P, S], F32)) for i in range(P1S)]
        ps_pv = ctx.enter_context(nc.psum_tensor("ps_pv", [P, S], F32))
        ps_w = [ctx.enter_context(nc.psum_tensor(f"ps_w{i}", [P, S], F32)) for i in range(2)]

        w_loaded = sem("w_loaded")
        const_zeroed = sem("const_zeroed")
        const_ready = sem("const_ready")
        ones_ready = sem("ones_ready")
        wo_permuted = sem("wo_permuted")
        w_transposed = sem("w_transposed")
        w_ready = sem("w_ready")
        x_ln_loaded = sem("x_ln_loaded")
        x_res_loaded = sem("x_res_loaded")
        xhat_ready = sem("xhat_ready")
        xT_in_psum = sem("xT_in_psum")
        xT_ready = sem("xT_ready")
        qkv_in_psum = sem("qkv_in_psum")
        hi_ready = sem("hi_ready")
        kvT_ready = sem("kvT_ready")
        resid_ready = sem("resid_ready")
        mid_ready = sem("mid_ready")
        lo_ready = sem("lo_ready")
        k_stacked = sem("k_stacked")
        q_stacked = sem("q_stacked")
        v_in_psum = sem("v_in_psum")
        v_ready = sem("v_ready")
        p1_in_psum = sem("p1_in_psum")
        p1_reduced = sem("p1_reduced")
        m_hi = sem("m_hi")
        m_res = sem("m_res")
        m_mid = sem("m_mid")
        m_split = sem("m_split")
        mT_in_psum = sem("mT_in_psum")
        mT_ready = sem("mT_ready")
        m_stacked = sem("m_stacked")
        st_in_psum = sem("st_in_psum")
        exp_done = sem("exp_done")
        masked = sem("masked")
        pv_done = sem("pv_done")
        oT_evacuated = sem("oT_evacuated")
        z_gathered = sem("z_gathered")
        o_gathered = sem("o_gathered")
        recip_done = sem("recip_done")
        r_rowed = sem("r_rowed")
        r_spread = sem("r_spread")
        o_normed = sem("o_normed")
        y_in_psum = sem("y_in_psum")
        tsum_ready = sem("tsum_ready")
        x2hat_ready = sem("x2hat_ready")
        x2T_in_psum = sem("x2T_in_psum")
        x2T_ready = sem("x2T_ready")
        f_in_psum = sem("f_in_psum")
        osum_ready = sem("osum_ready")
        bias4_ready = sem("bias4_ready")
        out_ready = sem("out_ready")
        out_stored = [sem("out_stored0"), sem("out_stored1")]

        def over_batches(eng, step, end=B - 2):
            step(0, 0, True, False)
            step(1, 1, True, True)
            with eng.Fori(2, end, 2) as b:
                step(b, 0, True, True)
                step(b + 1, 1, True, True)
            for b in range(end, B):
                step(b, b % 2, b + 1 < B, True)

        def worked_out(eng, count):
            return count if isinstance(count, int) else eng.snap(eng.to_reg(count))

        def p1_at(g, t):
            tiles = [t] if t < ST - 1 else [t, P1 - 1]
            return [((g + 2) // KVH, (g + 2) % KVH, tile) for tile in tiles]

        STEP = ST * KVH

        def late(name, slot, b):
            found = [b - 1] if slot == AT[name] and not (isinstance(b, int) and b < 1) else []
            return found + ([b - 2] if slot + STEP == AT[name] and not (isinstance(b, int) and b < 2) else [])

        mT_psum = ps_pv[:, 0:P // 2].bitcast(BF16)

        block = ctx.enter_context(nc.Block())

        @block.sync
        def _(sp):
            sp.dma_start(x_ln[:], x_v[0]).then_inc(x_ln_loaded, 16)
            sp.dma_start(wq_sb[:], wq.rearrange("(c p) i -> p c i", p=P)).then_inc(w_loaded, 16)
            sp.dma_start(wkv_sb[0:64, :], wk).then_inc(w_loaded, 16)
            sp.dma_start(wkv_sb[64:128, :], wv).then_inc(w_loaded, 16)
            sp.dma_start(wo_sb[:], wo.rearrange("(c p) i -> p c i", p=P)).then_inc(w_loaded, 16)
            sp.dma_start(wf_sb[:], wf.rearrange("(c p) i -> p c i", p=P)).then_inc(w_loaded, 16)
            sp.dma_start(dish2[0:R, :], disha).then_inc(w_loaded, 16)
            sp.dma_start(dish2[R:2 * R, :], disha).then_inc(w_loaded, 16)

            def stack_k_part(d, par, part):
                sp.wait_ge([hi_ready, mid_ready, lo_ready][part], 3 * d + 1)
                for n in range(len(K_PART)):
                    if K_PART[n] == part:
                        sp.dma_start(KS[DH * n:DH * (n + 1), par, :, :], k_split[:, part, :]).then_inc(k_stacked, 16)

            def stack_q_part(d, par, part):
                sp.wait_ge([hi_ready, mid_ready, lo_ready][part], 3 * d + 3)
                for n in range(len(Q_PART)):
                    if Q_PART[n] == part:
                        sp.dma_start(QS[DH * n:DH * (n + 1), par, :, :].rearrange("p (s m) t -> p s (m t)", m=2),
                                     q_split[:, part, :, :].rearrange("p m t -> p (m t)")).then_inc(q_stacked, 16)

            def stack_m(n, g, par):
                sp.wait_ge(mT_ready, n + 1)
                sp.dma_start(QS[KR:KM, par, HG * g:HG * (g + 1), :].rearrange("p h (t q) -> p (h t) q", q=P),
                             mT_sb[:, g % 2, :]).then_inc(m_stacked, 16)

            def gather_o(d, par):
                sp.wait_ge(oT_evacuated, 4 * d + 4)
                for c in range(HG):
                    sp.dma_start(oraw[64 * (c % 2):64 * (c % 2) + 64, c // 2, :],
                                 OT[32 * c:32 * c + DH, par, :, :]).then_inc(o_gathered, 16)

            def store_out(d, h):
                sp.wait_ge(out_ready, 2 * d + h + 3)
                sp.dma_start(out_v[d][:, 2 * h:2 * h + 2, :], outb[:, 2 * h:2 * h + 2, :]).then_inc(out_stored[h], 16)

            def load_x_res(d):
                if not (isinstance(d, int) and d == 0):
                    sp.wait_ge(tsum_ready, 2 * d)
                sp.dma_start(x_res[:], x_v[d]).then_inc(x_res_loaded, 16)

            def load_x_ln(d):
                sp.wait_ge(xhat_ready, d)
                sp.dma_start(x_ln[:], x_v[d]).then_inc(x_ln_loaded, 16)

            load_x_ln(1)
            stack_k_part(0, 0, HI)
            stack_k_part(0, 0, MID)
            stack_q_part(0, 0, HI)
            stack_k_part(0, 0, LO)
            stack_q_part(0, 0, MID)
            stack_q_part(0, 0, LO)
            stack_m(0, 0, 0)

            def step(b, par, nxt, prev):
                for slot in range(ST * KVH):
                    g, t = slot // ST, slot % ST
                    if prev:
                        if slot == AT["sp_x_res"]:
                            load_x_res(b - 1)
                        if slot == AT["sp_oraw"]:
                            gather_o(b - 1, 1 - par)
                    if slot == AT["sp_x_ln"] and (not isinstance(b, int) or b + 2 < B):
                        load_x_ln(b + 2)
                    if t == AT["sp_m"] and (g < 3 or nxt):
                        stack_m(4 * b + g + 1, (g + 1) % KVH, par if g < 3 else 1 - par)
                    if nxt:
                        for part in (HI, MID, LO):
                            if slot == AT["sp_k"][part]:
                                stack_k_part(b + 1, 1 - par, part)
                            if slot == AT["sp_q"][part]:
                                stack_q_part(b + 1, 1 - par, part)
                    for h in range(2):
                        for d in late(f"sp_out{h}", slot, b):
                            store_out(d, h)

            over_batches(sp, step, B - 4)
            load_x_res(B - 1)
            gather_o(B - 1, (B - 1) % 2)
            for h in range(2):
                if AT[f"sp_out{h}"] >= STEP:
                    store_out(B - 2, h)
            store_out(B - 1, 0)
            store_out(B - 1, 1)
            sp.wait_ge(out_stored[0], 16 * B + 16)
            sp.wait_ge(out_stored[1], 16 * B + 16)

        @block.tensor
        def _(pe):
            def transpose_weights():
                pe.wait_ge(const_ready, 5)
                pe.wait_ge(w_loaded, 16 * 7)
                for c in range(NC):
                    for o in range(2):
                        nc.tensor.transpose(ps_p1[0][:, D * c + P * o:D * c + P * (o + 1)],
                                            wq_sb[:, o, P * c:P * (c + 1)], identf[:])
                for c in range(NC):
                    nc.tensor.transpose(ps_p1[1][:, P * c:P * (c + 1)],
                                        wkv_sb[:, P * c:P * (c + 1)], identf[:]).then_inc(w_transposed, 1)
                pe.wait_ge(wo_permuted, 1)
                for c in range(NC):
                    for o in range(2):
                        nc.tensor.transpose(ps_p1[2][:, D * c + P * o:D * c + P * (o + 1)],
                                            wo_perm[:, o, P * c:P * (c + 1)], identf[:])
                for c in range(NC):
                    for o in range(2):
                        last = nc.tensor.transpose(ps_st[0][:, D * c + P * o:D * c + P * (o + 1)],
                                                   wf_sb[:, o, P * c:P * (c + 1)], identf[:])
                last.then_inc(w_transposed, 1)

            def transpose_x(d, c):
                pe.wait_ge(xhat_ready, d + 1)
                for t in range(NT):
                    last = nc.tensor.transpose(ps_w[c][:, P * t:P * (t + 1)], xhat[:, t, P * c:P * (c + 1)], identf[:])
                last.then_inc(xT_in_psum, 1)

            def project(bank, c, weights):
                last = nc.tensor.matmul(ps_w[bank][:], weights, xT[:, c, :], start=(c == 0), stop=(c == NC - 1),
                                        skip_group_check=True)
                if c == NC - 1:
                    last.then_inc(qkv_in_psum, 1)

            def project_kv(d, c):
                pe.wait_ge(xT_ready, 2 * d + 2)
                project(0, c, wkvT[:, c, :])

            def project_q0(d, c):
                project(1, c, wqT[:, c, 0:P])

            def project_q1(d, c):
                if c == 0:
                    pe.wait_ge(hi_ready, 3 * d + 1)
                project(0, c, wqT[:, c, P:2 * P])

            def transpose_v(d):
                pe.wait_ge(kvT_ready, d + 1)
                pe.wait_ge(resid_ready, 3 * d + 2)
                for t in range(NT):
                    last = nc.tensor.transpose(ps_w[1][:, P * t:P * (t + 1)], kvT_sb[:, P * t:P * (t + 1)], identf[:])
                last.then_inc(v_in_psum, 1)

            def p1_tile(d, g, tile, par):
                at = P1 * g + tile
                per = P1 * KVH
                if tile == 0:
                    if g == 0:
                        pe.wait_ge(k_stacked, 16 * len(K_PART) * (d + 1))
                        pe.wait_ge(q_stacked, 16 * len(Q_PART) * (d + 1))
                if at >= P1S:
                    pe.wait_ge(p1_reduced, per * d + at - P1S + 1)
                elif not (isinstance(d, int) and d == 0):
                    before = max(i for i in range(per) if i % P1S == at)
                    pe.wait_ge(p1_reduced, per * d + before + 1 - per)
                ps = ps_p1[at % P1S]
                if tile < 8:
                    qt, h = 3 - tile // HG, tile % HG
                    heads, n = [h], P * (qt + 1)
                elif tile < 10:
                    qt, heads, n = 1, [2 * (tile - 8), 2 * (tile - 8) + 1], 2 * P
                else:
                    qt, heads, n = 0, list(range(HG)), P
                for i, h in enumerate(heads):
                    nc.tensor.matmul(ps[:, n * i:n * (i + 1)], QS[0:KR, par, HG * g + h, P * qt:P * (qt + 1)],
                                     KS[0:KR, par, g, 0:n], start=(i == 0), stop=False, skip_group_check=True)
                k = len(heads)
                diag = ps[:, 0:n * k].rearrange("p (h k) -> p h k", h=k)[:, :, n - P:n]
                nc.tensor.matmul(diag, identb[:], causal[:].unsqueeze(1).broadcast_to([P, k, P]), start=False,
                                 stop=True, skip_group_check=True).then_inc(p1_in_psum, 1)

            def transpose_m(n):
                pe.wait_ge(m_split, n + 1)
                if not (isinstance(n, int) and n < 2):
                    pe.wait_ge(oT_evacuated, n - 1)
                nc.tensor.transpose(mT_psum, msplit[:].rearrange("p a b -> p (a b)"), identb[:]).then_inc(mT_in_psum, 1)

            def st_tile(b, g, t, par):
                at = ST * g + t
                if t == 0:
                    pe.wait_ge(m_stacked, 16 * (4 * b + g + 1))
                if not (isinstance(b, int) and b == 0 and at < 2):
                    pe.wait_ge(exp_done, ST * KVH * b + at - 1)
                ps = ps_st[t % 2]
                if t < HG:
                    last = nc.tensor.matmul(ps[:], KS[0:KM, par, g, 0:P], QS[0:KM, par, HG * g + t, :],
                                            start=True, stop=True)
                elif t < 2 * HG:
                    h = HG * g + t - HG
                    nc.tensor.matmul(ps[:, P:S], KS[0:KM, par, g, P:2 * P], QS[0:KM, par, h, P:S],
                                     start=True, stop=True)
                    last = nc.tensor.matmul(ps[:, 0:P], KS[0:KM, par, g, 3 * P:S], QS[0:KM, par, h, 3 * P:S],
                                            start=True, stop=True)
                else:
                    h = HG * g + 2 * (t - 2 * HG)
                    last = nc.tensor.matmul(ps[:].rearrange("p (h q) -> p h q", h=2), KS[0:KM, par, g, 2 * P:3 * P],
                                            QS[0:KM, par, h:h + 2, 2 * P:S], start=True, stop=True)
                last.then_inc(st_in_psum, 1)

            def pv(n, g, par, kt, v_count=None, bank_held=False):
                tile = {0: 0, 1: HG, 3: HG, 2: 2 * HG}[kt]
                pe.wait_ge(masked, 3 * n + {0: 1, 1: 2, 3: 2, 2: 3}[kt])
                if kt == 0:
                    if g == 0:
                        pe.wait_ge(v_ready, v_count)
                    if bank_held:
                        pe.wait_ge(mT_ready, n + 2)
                    else:
                        pe.wait_ge(oT_evacuated, n)
                for h in range(HG):
                    slot = ST * (g % 2) + tile + (h // 2 if kt == 2 else h)
                    lo = {0: 0, 1: P, 3: 0, 2: 2 * P * (h % 2)}[kt]
                    width = S - P * kt
                    last = nc.tensor.matmul(ps_pv[32 * h:32 * (h + 1), P * kt:S], V1[:, par, kt, g, :],
                                            PT[:, slot, lo:lo + width], start=(kt == 0), stop=(kt == 2),
                                            tile_position=(0, 32 * h), skip_group_check=True)
                if kt == 2:
                    last.then_inc(pv_done, 1)

            def out_project(d, h, t):
                if t == 0:
                    pe.wait_ge(o_normed, NC * (2 * d + h + 1))
                for c in range(NC):
                    last = nc.tensor.matmul(ps_w[h][:, D * t:D * (t + 1)],
                                            oT[:, c, P * (2 * h + t):P * (2 * h + t + 1)], woT[:, c, :],
                                            start=(c == 0), stop=(c == NC - 1), skip_group_check=True)
                if t == 1:
                    last.then_inc(y_in_psum, 1)

            def transpose_x2(d, h):
                pe.wait_ge(x2hat_ready, 2 * d + h + 1)
                for c in range(NC):
                    for t in range(2):
                        last = nc.tensor.transpose(ps_w[h][:, D * c + P * t:D * c + P * (t + 1)],
                                                   x2hat[:, 2 * h + t, P * c:P * (c + 1)], identf[:])
                last.then_inc(x2T_in_psum, 1)

            def ffn(d, h, t):
                if t == 0:
                    pe.wait_ge(x2T_ready, 2 * d + h + 1)
                for c in range(NC):
                    last = nc.tensor.matmul(ps_w[h][:, D * t:D * (t + 1)],
                                            x2T[:, c, P * (2 * h + t):P * (2 * h + t + 1)], wfT[:, c, :],
                                            start=(c == 0), stop=(c == NC - 1), skip_group_check=True)
                if t == 1:
                    last.then_inc(f_in_psum, 1)

            def keep_clock(rounds):
                with pe.Fori(0, rounds):
                    for _ in range(4):
                        nc.tensor.matmul(ps_p1[0][:], KS[0:KR, 0, 0, 0:P], QS[0:KR, 0, 0, :], start=True, stop=True)

            transpose_weights()
            for c in range(NC):
                transpose_x(0, c)
            pe.wait_ge(w_ready, 4)
            for project_part in (project_kv, project_q0, project_q1):
                for c in range(NC):
                    project_part(0, c)
            transpose_v(0)
            pe.wait_ge(ones_ready, 2)
            for tile in range(P1):
                p1_tile(0, 0, tile, 0)
            for tile in range(P1):
                p1_tile(0, 1, tile, 0)
                if tile == AT["pe_mT"]:
                    transpose_m(0)

            def step(b, par, nxt, prev):
                n0 = 4 * b
                first = isinstance(b, int) and b == 0
                for g in range(KVH):
                    n = n0 + g
                    for t in range(ST):
                        slot = ST * g + t
                        st_tile(b, g, t, par)
                        for ahead, pg, tile in p1_at(g, t):
                            if ahead == 0 or nxt:
                                p1_tile(b + ahead, pg, tile, par if ahead == 0 else 1 - par)
                        if not (first and g == 0):
                            for kt in (1, 3, 2):
                                if t == AT[f"pe_pv{kt}"]:
                                    pv(n - 1, (g - 1) % KVH, par if g else 1 - par, kt)
                        if t == AT["pe_mT"] and (g < 3 or nxt):
                            transpose_m(n + 1)
                        if t == AT["pe_pv0"]:
                            pv(n, g, par, 0, b + 1, g < 3 or nxt)
                        if nxt:
                            if slot == AT["pe_xT0"]:
                                if prev:
                                    pe.wait_ge(osum_ready, 2 * b - 1)
                                transpose_x(b + 1, 0)
                            if slot == AT["pe_xT1"]:
                                if prev:
                                    pe.wait_ge(osum_ready, 2 * b)
                                else:
                                    pe.wait_ge(v_ready, 1)
                                transpose_x(b + 1, 1)
                            for c in range(NC):
                                if slot == AT[f"pe_kv{c}"]:
                                    project_kv(b + 1, c)
                                if slot == AT[f"pe_q0{c}"]:
                                    project_q0(b + 1, c)
                                if slot == AT[f"pe_q1{c}"]:
                                    project_q1(b + 1, c)
                            if slot == AT["pe_v"]:
                                transpose_v(b + 1)
                        if prev:
                            for i in range(NT):
                                if slot == AT[f"pe_y{i}"]:
                                    if i == 0 and nxt:
                                        pe.wait_ge(resid_ready, 3 * (b + 1) + 3)
                                    if i == 0 and not nxt:
                                        pe.wait_ge(osum_ready, 2 * b - 1)
                                    if i == 2 and nxt:
                                        pe.wait_ge(v_ready, b + 2)
                                    if i == 2 and not nxt:
                                        pe.wait_ge(osum_ready, 2 * b)
                                    out_project(b - 1, i // 2, i % 2)
                            for h in range(2):
                                if slot == AT[f"pe_x2T{h}"]:
                                    transpose_x2(b - 1, h)
                            for i in range(NT):
                                if slot == AT[f"pe_ffn{i}"]:
                                    ffn(b - 1, i // 2, i % 2)

            over_batches(pe, step)
            last_g, last_par = KVH - 1, (B - 1) % 2
            for kt in (1, 3, 2):
                pv(KVH * B - 1, last_g, last_par, kt)
            pe.wait_ge(p1_reduced, P1 * KVH * B)
            keep_clock(15)
            pe.wait_ge(osum_ready, 2 * (B - 1) + 2)
            for i in range(NT):
                out_project(B - 1, i // 2, i % 2)
            keep_clock(8)
            for h in range(2):
                transpose_x2(B - 1, h)
                for t in range(2):
                    ffn(B - 1, h, t)

        @block.scalar
        def _(act):
            def copy_xT(d, c):
                act.wait_ge(xT_in_psum, 2 * d + c + 1)
                nc.scalar.copy(xT[:, c, :], ps_w[c][:]).then_inc(xT_ready, 1)

            def split_hi_k(d):
                act.wait_ge(qkv_in_psum, 3 * d + 1)
                if not (isinstance(d, int) and d == 0):
                    act.wait_ge(k_stacked, 16 * len(K_PART) * d)
                nc.scalar.copy(kvT_sb[:], ps_w[0][:]).then_inc(kvT_ready, 1)
                nc.scalar.copy(k_split[:, HI, :], ps_w[0][0:64, :]).then_inc(hi_ready, 1)

            def split_hi_q(d, half):
                act.wait_ge(qkv_in_psum, 3 * d + 2 + half)
                if not (isinstance(d, int) and d == 0):
                    act.wait_ge(q_stacked, 16 * len(Q_PART) * d)
                nc.scalar.mul(q_split[:, HI, half, :], ps_w[1 - half][:], SCALE).then_inc(hi_ready, 1)

            def split_mid(d, i):
                act.wait_ge(resid_ready, 3 * d + i + 1)
                rows, mid = (64, k_split[:, MID, :]) if i == 0 else (P, q_split[:, MID, i - 1, :])
                nc.scalar.copy(mid, resid[0:rows, i, :]).then_inc(mid_ready, 1)

            def copy_v(d, par):
                act.wait_ge(v_in_psum, d + 1)
                nc.scalar.copy(V1[:, par, :, :, 0:DH],
                               ps_w[1][:].rearrange("p (t k g d) -> p t k g d", t=NT, k=2, d=DH)[:, :, 1]
                               ).then_inc(v_ready, 1)

            def copy_mT(n, g):
                act.wait_ge(mT_in_psum, n + 1)
                if not (isinstance(n, int) and n < 2):
                    act.wait_ge(m_stacked, 16 * (n - 1))
                nc.scalar.copy(mT_sb[:, g % 2, :], mT_psum[0:3 * H, :]).then_inc(mT_ready, 1)

            def exp_tile(b, g, t):
                act.wait_ge(st_in_psum, ST * (KVH * b + g) + t + 1)
                if t == 0 and not (isinstance(b, int) and b == 0 and g < 2):
                    act.wait_ge(pv_done, 4 * b + g - 1)
                nc.scalar.activation(PT[:, ST * (g % 2) + t, :], ps_st[t % 2][:], ACT.Exp).then_inc(exp_done, 1)

            def copy_oT(n, g, par, d):
                act.wait_ge(pv_done, n + 1)
                if g == 0 and not (isinstance(d, int) and d < 2):
                    act.wait_ge(z_gathered, 16 * (d - 1))
                    act.wait_ge(o_gathered, 64 * (d - 1))
                nc.scalar.copy(OT[:, par, g, :], ps_pv[:]).then_inc(oT_evacuated, 1)

            def gather_z(d, par):
                act.wait_ge(oT_evacuated, 4 * d + 4)
                act.dma_start(zc[:], OT[DH:P:2 * DH, par, :, :].rearrange("p g t -> p (g t)")).then_inc(z_gathered, 16)

            def row_r(d):
                act.wait_ge(recip_done, d + 1)
                act.dma_start(r_dram.rearrange("c (k e) -> (c k) e", e=64), rc[:]).then_inc(r_rowed, 16)

            def spread_r(d):
                act.wait_ge(r_rowed, 16 * (d + 1))
                for c in range(HG):
                    act.dma_start(rrep[64 * (c % 2):64 * (c % 2) + 64, c // 2, :],
                                  r_dram[c].unsqueeze(0).broadcast_to([DH, KVH * S])).then_inc(r_spread, 16)

            def apply_ln3(d, h):
                act.wait_ge(ln3.shift_done, 2 * d + h + 1)
                for t in (2 * h, 2 * h + 1):
                    last = nc.scalar.activation(x2hat[:, t, :], tsum[:, t, :], ACT.Identity,
                                                bias=ln3.shift[:, t:t + 1], scale=ln3.rstd[:, t:t + 1])
                last.then_inc(x2hat_ready, 1)

            def copy_x2T(d, h):
                act.wait_ge(x2T_in_psum, 2 * d + h + 1)
                nc.scalar.copy(x2T[:, :, 2 * P * h:2 * P * (h + 1)],
                               ps_w[h][:].rearrange("p (c q) -> p c q", c=NC)).then_inc(x2T_ready, 1)

            def scale_f(d, h):
                act.wait_ge(bias4_ready, 2 * d + h + 1)
                if not (isinstance(d, int) and d == 0):
                    act.wait_ge(out_ready, 2 * d + h + 1)
                for t in (2 * h, 2 * h + 1):
                    last = nc.scalar.activation(osum[:, t, :], ps_w[h][:, D * (t % 2):D * (t % 2 + 1)], ACT.Identity,
                                                bias=bias4[:, t:t + 1], scale=ln4.rstd[:, t:t + 1])
                last.then_inc(osum_ready, 1)

            act.sem_inc(osum_ready, 2)
            act.sem_inc(out_ready, 2)
            for h in range(2):
                act.sem_inc(out_stored[h], 16)
            act.wait_ge(w_transposed, 3)
            nc.scalar.copy(woT[:].rearrange("p c o -> p (c o)"), ps_p1[2][:]).then_inc(w_ready, 1)
            copy_xT(0, 0)
            copy_xT(0, 1)
            split_hi_k(0)
            split_hi_q(0, 0)
            split_mid(0, 0)
            split_hi_q(0, 1)
            split_mid(0, 1)
            copy_v(0, 0)
            split_mid(0, 2)
            copy_mT(0, 0)

            def step(b, par, nxt, prev):
                n0 = 4 * b
                first = isinstance(b, int) and b == 0
                for g in range(KVH):
                    for t in range(ST):
                        slot = ST * g + t
                        exp_tile(b, g, t)
                        if t == AT["act_oT"] and not (first and g == 0):
                            copy_oT(n0 + g - 1, (g - 1) % KVH, par if g else 1 - par, b if g else b - 1)
                        if t == AT["act_mT"] and (g < 3 or nxt):
                            copy_mT(n0 + g + 1, (g + 1) % KVH)
                        if nxt:
                            for c in range(NC):
                                if slot == AT[f"act_xT{c}"]:
                                    copy_xT(b + 1, c)
                            if slot == AT["act_k"]:
                                split_hi_k(b + 1)
                            for half in range(2):
                                if slot == AT[f"act_q{half}"]:
                                    split_hi_q(b + 1, half)
                            for i in range(3):
                                if slot == AT[f"act_mid{i}"]:
                                    split_mid(b + 1, i)
                            if slot == AT["act_v"]:
                                copy_v(b + 1, 1 - par)
                        if prev:
                            if slot == AT["act_z"]:
                                gather_z(b - 1, 1 - par)
                            if slot == AT["act_row"]:
                                row_r(b - 1)
                            if slot == AT["act_spread"]:
                                spread_r(b - 1)
                            for h in range(2):
                                if slot == AT[f"act_ln3_{h}"]:
                                    apply_ln3(b - 1, h)
                                if slot == AT[f"act_x2T{h}"]:
                                    copy_x2T(b - 1, h)
                        for h in range(2):
                            for d in late(f"act_out{h}", slot, b):
                                scale_f(d, h)

            over_batches(act, step)
            copy_oT(KVH * B - 1, KVH - 1, (B - 1) % 2, B - 1)
            gather_z(B - 1, (B - 1) % 2)
            for h in range(2):
                if AT[f"act_out{h}"] >= STEP:
                    scale_f(B - 2, h)
            row_r(B - 1)
            spread_r(B - 1)
            for h in range(2):
                apply_ln3(B - 1, h)
                copy_x2T(B - 1, h)
            scale_f(B - 1, 0)
            scale_f(B - 1, 1)

        @block.vector
        def _(dve):
            def constants():
                nc.vector.memset(powexp[:], -0.5).then_inc(const_ready, 1)
                nc.vector.memset(msplit[:], 0.0).then_inc(const_ready, 1)

            def ones():
                nc.vector.memset(V1[:, :, :, :, DH:2 * DH], 1.0).then_inc(ones_ready, 1)
                nc.vector.memset(KS[KR:KM], 1.0).then_inc(ones_ready, 1)

            def permute_wo():
                dve.wait_ge(w_loaded, 16 * 7)
                for o in range(2):
                    for cc in range(NC):
                        src = wo_sb[:, o, :].rearrange("p (g c d) -> p c d g", g=KVH, c=HG)[:, 2 * cc:2 * cc + 2, :, :]
                        dst = wo_perm[:, o, P * cc:P * (cc + 1)].rearrange("p (c d g) -> p c d g", c=2, d=DH)
                        last = nc.vector.tensor_copy(dst, src)
                last.then_inc(wo_permuted, 1)

            def lay_out_weights():
                dve.wait_ge(w_transposed, 2)
                for c in range(NC):
                    nc.vector.tensor_copy(
                        wqT[:, c, :].rearrange("p (m d s) -> p m d s", m=2, d=DH),
                        ps_p1[0][:, D * c:D * (c + 1)].rearrange("p (s m d) -> p m d s", s=8, m=2))
                dve.wait_ge(w_transposed, 2)
                for c in range(NC):
                    nc.vector.tensor_copy(wkvT[:, c, 0:64].rearrange("p (d g) -> p d g", d=DH),
                                          ps_p1[1][:, P * c:P * c + 64].rearrange("p (g d) -> p d g", g=KVH))
                    last = nc.vector.tensor_copy(wkvT[:, c, 64:P], ps_p1[1][:, P * c + 64:P * (c + 1)])
                last.then_inc(w_ready, 2)
                dve.wait_ge(w_transposed, 3)
                nc.vector.tensor_tensor(wfT[:], ps_st[0][:].rearrange("p (c o) -> p c o", c=NC),
                                        dish2[:].unsqueeze(1).broadcast_to([P, NC, D]), ALU.add).then_inc(w_ready, 1)

            def stats(ln, src, h):
                for t in (2 * h, 2 * h + 1):
                    last = nc.vector.bn_stats(ln.stats[:, t, :], src(t))
                last.then_inc(ln.stats_done, 1)

            def aggregate(ln, d, h):
                done_by = worked_out(dve, 2 * d + h + 1)
                dve.wait_ge(x_ln_loaded, 16)
                dve.wait_ge(ln.stats_done, done_by)
                for t in (2 * h, 2 * h + 1):
                    last = nc.vector.bn_aggr(ln.mv[:, t, :], ln.stats[:, t, :])
                last.then_inc(ln.var_done, 1)

            def shift(ln, h, done):
                a, b = 2 * h, 2 * h + 2
                dve.wait_ge(ln.rstd_done, done + 1)
                nc.vector.scalar_tensor_tensor(ln.shift[:, a:b], ln.mv[:, a:b, 0], -1.0, ln.rstd[:, a:b],
                                               ALU.mult, ALU.mult).then_inc(ln.shift_done, 1)

            def ln1_stats(d, h):
                if h == 0:
                    dve.wait_ge(x_ln_loaded, 16 * (d + 1))
                stats(ln1, lambda t: x_ln[:, t, :], h)

            def ln1_apply(d, h):
                if h == 0:
                    dve.wait_ge(ln1.rstd_done, d + 1)
                    if not (isinstance(d, int) and d == 0):
                        dve.wait_ge(xT_in_psum, 2 * d)
                for t in (2 * h, 2 * h + 1):
                    last = nc.vector.tensor_scalar(xhat[:, t, :], x_ln[:, t, :], ln1.mv[:, t, 0:1],
                                                   ln1.rstd[:, t:t + 1], ALU.subtract, ALU.mult)
                if h == 1:
                    last.then_inc(xhat_ready, 1)

            def split_rest(d, i):
                dve.wait_ge(hi_ready, 3 * d + i + 1)
                if i == 0:
                    rows, ps, scale, part = 64, kvT_sb, 1.0, lambda p: k_split[:, p, :]
                    dve.wait_ge(kvT_ready, d + 1)
                else:
                    rows, ps, scale = P, ps_w[2 - i], SCALE
                    part = lambda p: q_split[:, p, i - 1, :]
                if not (isinstance(d, int) and d == 0):
                    dve.wait_ge(lo_ready, 3 * d + i - 2)
                nc.vector.scalar_tensor_tensor(resid[0:rows, i, :], ps[0:rows, :], scale, part(HI),
                                               ALU.mult, ALU.subtract).then_inc(resid_ready, 1)

            def p1_reduce(d, g, tile):
                at = P1 * g + tile
                n = 4 * d + g
                if tile == 0 and not (isinstance(d, int) and d == 0 and g < 2):
                    dve.wait_ge(m_split, n - 1)
                dve.wait_ge(p1_in_psum, P1 * n + tile + 1)
                ps = ps_p1[at % P1S]
                if tile < 8:
                    qt, h0, k = 3 - tile // HG, tile % HG, 1
                elif tile < 10:
                    qt, h0, k = 1, 2 * (tile - 8), 2
                else:
                    qt, h0, k = 0, 0, HG
                w = P * (qt + 1)
                m = mneg[:, g % 2, :].rearrange("p (h t) -> p h t", h=HG)[:, h0:h0 + k, qt]
                nc.vector.tensor_reduce(m, ps[:, 0:w * k].rearrange("p (h k) -> p h k", h=k), AX.X, ALU.max,
                                        negate=True).then_inc(p1_reduced, 1)

            def recip(d):
                dve.wait_ge(z_gathered, 16 * (d + 1))
                if not (isinstance(d, int) and d == 0):
                    dve.wait_ge(r_rowed, 16 * d)
                nc.vector.reciprocal(rc[:], zc[:]).then_inc(recip_done, 1)

            def ln2_stats(d, h):
                dve.wait_ge(y_in_psum, 2 * d + h + 1)
                stats(ln2, lambda t: ps_w[h][:, D * (t % 2):D * (t % 2 + 1)], h)

            def ln2_apply(d, h):
                if h == 0:
                    dve.wait_ge(x_res_loaded, 16 * (d + 1))
                    if not (isinstance(d, int) and d == 0):
                        dve.wait_ge(x2hat_ready, 2 * d)
                        dve.wait_ge(out_ready, 2 * d + 2)
                dve.wait_ge(ln2.rstd_done, 2 * d + h + 1)
                for t in (2 * h, 2 * h + 1):
                    last = nc.vector.scalar_tensor_tensor(tsum[:, t, :], ps_w[h][:, D * (t % 2):D * (t % 2 + 1)],
                                                          ln2.rstd[:, t:t + 1], x_res[:, t, :], ALU.mult, ALU.add)
                last.then_inc(tsum_ready, 1)
                shift(ln2, h, 2 * d + h)

            def ln3_stats(d, h):
                dve.wait_ge(tsum_ready, 2 * d + h + 1)
                stats(ln3, lambda t: tsum[:, t, :], h)

            def ln4_stats(d, h):
                dve.wait_ge(f_in_psum, 2 * d + h + 1)
                stats(ln4, lambda t: ps_w[h][:, D * (t % 2):D * (t % 2 + 1)], h)

            def ln4_shift(d, h):
                shift(ln4, h, 2 * d + h)

            def add_shifts(d, h):
                a, b = 2 * h, 2 * h + 2
                dve.wait_ge(ln4.shift_done, 2 * d + h + 1)
                if not (isinstance(d, int) and d == 0):
                    dve.wait_ge(osum_ready, 2 * d + h + 1)
                nc.vector.tensor_tensor(bias4[:, a:b], ln4.shift[:, a:b], ln2.shift[:, a:b],
                                        ALU.add).then_inc(bias4_ready, 1)

            constants()
            for h in range(2):
                ln1_stats(0, h)
            for h in range(2):
                aggregate(ln1, 0, h)
            permute_wo()
            for h in range(2):
                ln1_apply(0, h)
            lay_out_weights()
            ones()
            for i in range(3):
                split_rest(0, i)
            for h in range(2):
                ln1_stats(1, h)
            for h in range(2):
                aggregate(ln1, 1, h)
            for tile in range(P1):
                p1_reduce(0, 0, tile)
            for tile in range(P1):
                p1_reduce(0, 1, tile)
            for h in range(2):
                ln1_apply(1, h)

            def step(b, par, nxt, prev):
                for g in range(KVH):
                    for t in range(ST):
                        slot = ST * g + t
                        for ahead, pg, tile in p1_at(g, t):
                            if ahead == 0 or nxt:
                                p1_reduce(b + ahead, pg, tile)
                        if nxt:
                            for i, name in enumerate(("dve_k", "dve_q0", "dve_q1")):
                                if slot == AT[name]:
                                    split_rest(b + 1, i)
                        for h in range(2):
                            if prev:
                                if h == 0 and slot == AT["dve_recip"]:
                                    recip(b - 1)
                                if slot == AT[f"dve_ln2_{h}"]:
                                    ln2_stats(b - 1, h)
                                if slot == AT[f"dve_ag2_{h}"]:
                                    aggregate(ln2, b - 1, h)
                                if slot == AT[f"dve_tsum{h}"]:
                                    ln2_apply(b - 1, h)
                                if slot == AT[f"dve_ln3_{h}"]:
                                    ln3_stats(b - 1, h)
                                if slot == AT[f"dve_ag3_{h}"]:
                                    aggregate(ln3, b - 1, h)
                                if slot == AT[f"dve_sh3_{h}"]:
                                    shift(ln3, h, 2 * (b - 1) + h)
                            for d in late(f"dve_ln4_{h}", slot, b):
                                ln4_stats(d, h)
                            for d in late(f"dve_ag4_{h}", slot, b):
                                aggregate(ln4, d, h)
                            for d in late(f"dve_sh4_{h}", slot, b):
                                ln4_shift(d, h)
                            for d in late(f"dve_bias{h}", slot, b):
                                add_shifts(d, h)
                            if not isinstance(b, int) or b + 2 < B:
                                if slot == AT[f"dve_ln1_{h}"]:
                                    ln1_stats(b + 2, h)
                                if slot == AT[f"dve_ag1_{h}"]:
                                    aggregate(ln1, b + 2, h)
                                if slot == AT[f"dve_xhat{h}"]:
                                    ln1_apply(b + 2, h)

            over_batches(dve, step)
            for h in range(2):
                if AT[f"dve_ln4_{h}"] >= STEP:
                    ln4_stats(B - 2, h)
                if AT[f"dve_ag4_{h}"] >= STEP:
                    aggregate(ln4, B - 2, h)
                if AT[f"dve_sh4_{h}"] >= STEP:
                    ln4_shift(B - 2, h)
                if AT[f"dve_bias{h}"] >= STEP:
                    add_shifts(B - 2, h)
            recip(B - 1)
            for h in range(2):
                ln2_stats(B - 1, h)
                aggregate(ln2, B - 1, h)
            ln2_apply(B - 1, 0)
            ln3_stats(B - 1, 0)
            aggregate(ln3, B - 1, 0)
            ln2_apply(B - 1, 1)
            shift(ln3, 0, 2 * (B - 1))
            ln3_stats(B - 1, 1)
            aggregate(ln3, B - 1, 1)
            shift(ln3, 1, 2 * (B - 1) + 1)
            for h in range(2):
                ln4_stats(B - 1, h)
                aggregate(ln4, B - 1, h)
                ln4_shift(B - 1, h)
                add_shifts(B - 1, h)

        @block.gpsimd
        def _(pool):
            def constants():
                nc.gpsimd.memset(identf[:], 0.0).then_inc(const_zeroed, 1)
                nc.gpsimd.memset(identb[:], 0.0).then_inc(const_zeroed, 1)
                nc.gpsimd.memset(causal[:], 0.0).then_inc(const_zeroed, 1)
                pool.wait_ge(const_zeroed, 3)
                for m in (identf, identb):
                    nc.gpsimd.affine_select(out=m[:], in_=m[:], compare_op=ALU.not_equal, fill=1.0, base=0,
                                            pattern=[[-1, P]], channel_multiplier=1).then_inc(const_ready, 1)
                nc.gpsimd.affine_select(out=causal[:], in_=causal[:], compare_op=ALU.is_ge, fill=NEG, base=0,
                                        pattern=[[-1, P]], channel_multiplier=1).then_inc(const_ready, 1)

            def rstd(ln, tiles, done):
                a, b = tiles
                done_by = worked_out(pool, (2 if ln is ln1 else 1) * (done + 1))
                pool.wait_ge(const_ready, 5)
                pool.wait_ge(ln.var_done, done_by)
                nc.gpsimd.tensor_scalar(ln.veps[:, a:b], ln.mv[:, a:b, 1], EPS, None,
                                        ALU.add).then_inc(ln.eps_done, 1)
                pool.wait_ge(ln.eps_done, done + 1)
                nc.gpsimd.tensor_tensor(ln.rstd[:, a:b], ln.veps[:, a:b], powexp[:, a:b],
                                        ALU.pow).then_inc(ln.rstd_done, 1)

            def split_lo(d, i):
                pool.wait_ge(mid_ready, 3 * d + i + 1)
                rows = 64 if i == 0 else P
                part = (lambda p: k_split[:, p, :]) if i == 0 else (lambda p: q_split[:, p, i - 1, :])
                nc.gpsimd.tensor_tensor(part(LO), resid[0:rows, i, :], part(MID), ALU.subtract).then_inc(lo_ready, 1)

            def split_max(n, g):
                maxima_by, parts_by = worked_out(pool, P1 * (n + 1)), worked_out(pool, n)
                pool.wait_ge(const_ready, 5)
                pool.wait_ge(p1_reduced, maxima_by)
                if not (isinstance(n, int) and n == 0):
                    pool.wait_ge(mT_in_psum, parts_by)
                m = mneg[:, g % 2, :]
                nc.gpsimd.tensor_copy(msplit[:, HI, :], m).then_inc(m_hi, 1)
                pool.wait_ge(m_hi, n + 1)
                nc.gpsimd.tensor_tensor(mres[:], m, msplit[:, HI, :], ALU.subtract).then_inc(m_res, 1)
                done_by = worked_out(pool, n + 1)
                pool.wait_ge(const_ready, 5)
                pool.wait_ge(m_res, done_by)
                nc.gpsimd.tensor_copy(msplit[:, MID, :], mres[:]).then_inc(m_mid, 1)
                pool.wait_ge(m_mid, n + 1)
                nc.gpsimd.tensor_tensor(msplit[:, LO, :], mres[:], msplit[:, MID, :], ALU.subtract).then_inc(m_split, 1)

            def mask(n, g, kind):
                s0 = ST * (g % 2)
                first, count = [(0, HG), (HG, HG), (2 * HG, 2)][kind]
                done_by = worked_out(pool, ST * n + first + count)
                pool.wait_ge(const_ready, 5)
                pool.wait_ge(exp_done, done_by)
                v = PT[:, s0 + first:s0 + first + count, :]
                if kind == 0:
                    v, blocks = v[:, :, 0:P], HG
                elif kind == 1:
                    v, blocks = v[:, :, 0:2 * P], 2 * HG
                else:
                    v, blocks = v.rearrange("p s (a q) -> p (s a) q", a=2)[:, :, 0:P], HG
                nc.gpsimd.affine_select(out=v, in_=v, compare_op=ALU.is_ge, fill=0.0, base=0,
                                        pattern=[[0, blocks], [1, P]],
                                        channel_multiplier=-1).then_inc(masked, 1)

            def norm_o(d, h):
                pool.wait_ge(r_spread, 64 * (d + 1))
                pool.wait_ge(o_gathered, 64 * (d + 1))
                if not (isinstance(d, int) and d == 0):
                    pool.wait_ge(y_in_psum, 2 * d)
                tokens = slice(2 * P * h, 2 * P * (h + 1))
                for c in range(NC):
                    nc.gpsimd.tensor_tensor(oT[:, c, tokens], oraw[:, c, tokens], rrep[:, c, tokens],
                                            ALU.mult).then_inc(o_normed, 1)

            def finish_out(d, h):
                tiles = slice(2 * h, 2 * h + 2)
                pool.wait_ge(osum_ready, 2 * d + h + 3)
                if not (isinstance(d, int) and d == 0):
                    pool.wait_ge(out_stored[h], 16 * d + 16)
                nc.gpsimd.tensor_tensor(outb[:, tiles, :], osum[:, tiles, :], tsum[:, tiles, :],
                                        ALU.add).then_inc(out_ready, 1)

            constants()
            rstd(ln1, (0, NT), 0)
            for i in range(3):
                split_lo(0, i)
            rstd(ln1, (0, NT), 1)
            split_max(0, 0)

            def step(b, par, nxt, prev):
                for g in range(KVH):
                    n = 4 * b + g
                    for t in range(ST):
                        slot = ST * g + t
                        if t == AT["pool_m"] and (g < 3 or nxt):
                            split_max(n + 1, (g + 1) % KVH)
                        for kind in range(3):
                            if t == AT["pool_ABC"][kind]:
                                mask(n, g, kind)
                        if nxt:
                            for i, name in enumerate(("pool_k", "pool_q0", "pool_q1")):
                                if slot == AT[name]:
                                    split_lo(b + 1, i)
                        for h in range(2):
                            if prev:
                                if slot == AT[f"pool_o{h}"]:
                                    norm_o(b - 1, h)
                                if slot == AT[f"pool_ln2_{h}"]:
                                    rstd(ln2, (2 * h, 2 * h + 2), 2 * (b - 1) + h)
                                if slot == AT[f"pool_ln3_{h}"]:
                                    rstd(ln3, (2 * h, 2 * h + 2), 2 * (b - 1) + h)
                            for d in late(f"pool_ln4_{h}", slot, b):
                                rstd(ln4, (2 * h, 2 * h + 2), 2 * d + h)
                            for d in late(f"pool_out{h}", slot, b):
                                finish_out(d, h)
                            if h == 0 and slot == AT["pool_ln1"] and (not isinstance(b, int) or b + 2 < B):
                                rstd(ln1, (0, NT), b + 2)

            over_batches(pool, step)
            for h in range(2):
                if AT[f"pool_ln4_{h}"] >= STEP:
                    rstd(ln4, (2 * h, 2 * h + 2), 2 * (B - 2) + h)
                if AT[f"pool_out{h}"] >= STEP:
                    finish_out(B - 2, h)
            for h in range(2):
                norm_o(B - 1, h)
            for h in range(2):
                rstd(ln2, (2 * h, 2 * h + 2), 2 * (B - 1) + h)
            for h in range(2):
                rstd(ln3, (2 * h, 2 * h + 2), 2 * (B - 1) + h)
            for h in range(2):
                rstd(ln4, (2 * h, 2 * h + 2), 2 * (B - 1) + h)
                finish_out(B - 1, h)


_INS = ["L0_attn_x", "L0_attn_Wq", "L0_attn_Wk", "L0_attn_Wv", "L0_attn_Wo", "L0_ffn_weight", "L0_ffn_disha"]


def kernel(**inputs):
    import numpy as np
    import concourse.bacc as bacc
    from concourse.bass_utils import run_bass_kernel_spmd

    nc = bacc.Bacc("TRN2", target_bir_lowering=False, num_devices=1)
    arrays, args = {}, []
    for name in _INS:
        a = np.ascontiguousarray(inputs[name])
        arrays[name] = a
        args.append(nc.dram_tensor(name, a.shape, mybir.dt.from_np(a.dtype), kind="ExternalInput").ap())
    shape = inputs["L0_attn_x"].shape
    out = nc.dram_tensor("block_out", shape, mybir.dt.float32, kind="ExternalOutput").ap()
    sandwich_kernel(nc, *args, out)
    return run_bass_kernel_spmd(nc, [arrays], core_ids=[0]).results[0]["block_out"]
```
